# Optimizing a Trainium2 kernel written in Bass

```python
import numpy as np
import jax
import jax.numpy as jnp

def _softmax(x, axis=-1):
    return jax.nn.softmax(x, axis=axis)

def _gelu(x):
    return jax.nn.gelu(x, approximate=True)

def _silu(x):
    return jax.nn.silu(x)

def _sigmoid(x):
    return jax.nn.sigmoid(x)

def _layernorm(x, axis=-1, eps=1e-05):
    m = jnp.mean(x, axis=axis, keepdims=True)
    v = jnp.var(x, axis=axis, keepdims=True)
    return (x - m) / jnp.sqrt(v + eps)

def _scatter_add(tgt, idx, src, axis=0):
    return tgt.at[idx].add(src)

def _segment_sum(src, seg, n):
    return jax.ops.segment_sum(src, seg, n)
kernel_name = 'mk_audio_tower_d1_tok_audfeat1024_r4_bc4ad7'

def setup_inputs(seed: int=0):
    np.random.seed(seed)
    _w = jnp.asarray

    def _rec_inputs():
        import jax
        import jax.numpy as jnp
        _rk = jax.random.key(seed)
        x = 0.00021031 + 1.00007 * jax.random.normal(jax.random.fold_in(_rk, 1), (16, 750, 256), jnp.float32)
        return x
    x = _rec_inputs()

    def _L0_tok_setup():
        import jax, jax.numpy as jnp
        import numpy as np
        DB4_DEC_LO = np.array([-0.010597401784997278, 0.032883011666982945, 0.030841381835986965, -0.18703481171888114, -0.02798376941698385, 0.6308807679295904, 0.7148465705525415, 0.23037781330885523], dtype=np.float64)
        NUM_LEVELS = 2

        def _afb1d_low(y, h0):
            B, D, N = y.shape
            L = h0.shape[0]
            outsize = (N + L - 1) // 2
            p = 2 * (outsize - 1) - N + L
            yp = jnp.pad(y, ((0, 0), (0, 0), (p // 2, p - p // 2)))
            k = jnp.broadcast_to(h0[None, None, :], (D, 1, L))
            return jax.lax.conv_general_dilated(yp, k, window_strides=(2,), padding='VALID', dimension_numbers=('NCH', 'OIH', 'NCH'), feature_group_count=D)
        key = jax.random.key(seed)
        x = jax.random.normal(key, (8, 1024, 256), dtype=jnp.float32)
        h0 = jnp.asarray(DB4_DEC_LO[::-1].copy(), dtype=jnp.float32)
        return {'x': x, 'h0': h0}
    _L0_tok_all = _L0_tok_setup()
    _L0_tok_in = {k: v for k, v in _L0_tok_all.items() if k in ('h0',)}
    del _L0_tok_all

    def _L0_attn_setup():
        import jax, jax.numpy as jnp
        import numpy as np
        NUM_HEADS = 32
        EPS = 1e-15
        key = jax.random.key(seed)
        k1, k2, k3, k4 = jax.random.split(key, 4)
        B, N, C = (8, 1024, 256)
        x = jax.random.normal(k1, (B, N, C), dtype=jnp.float32)
        qkv_weight = jax.random.normal(k2, (3 * C, C), dtype=jnp.float32) * C ** (-0.5)
        proj_weight = jax.random.normal(k3, (C, C), dtype=jnp.float32) * C ** (-0.5)
        proj_bias = jax.random.normal(k4, (C,), dtype=jnp.float32) * 0.01
        return {'x': x, 'qkv_weight': qkv_weight, 'proj_weight': proj_weight, 'proj_bias': proj_bias}
    _L0_attn_all = _L0_attn_setup()
    _L0_attn_in = {k: v for k, v in _L0_attn_all.items() if k in ('qkv_weight', 'proj_weight', 'proj_bias')}
    del _L0_attn_all

    def _L0_ffn_setup():
        import jax, jax.numpy as jnp
        import numpy as np
        B, S, H, E = (2, 2048, 256, 8)
        SCALE = 0.5
        key = jax.random.key(seed)
        k1, k2 = jax.random.split(key)
        x = jax.random.normal(k1, (B, S, H), dtype=jnp.float32)
        gate_w = jax.random.normal(k2, (E, H), dtype=jnp.float32) * 0.02
        coeff = SCALE * (1.0 + 0.05 * jnp.arange(E, dtype=jnp.float32))
        expert_w = coeff[:, None, None] * jnp.eye(H, dtype=jnp.float32)
        return {'x': x, 'gate_w': gate_w, 'expert_w': expert_w}
    _L0_ffn_all = _L0_ffn_setup()
    _L0_ffn_in = {k: v for k, v in _L0_ffn_all.items() if k in ('gate_w', 'expert_w')}
    del _L0_ffn_all
    return {'x': x, 'L0_tok_h0': _L0_tok_in['h0'], 'L0_attn_qkv_weight': _L0_attn_in['qkv_weight'], 'L0_attn_proj_weight': _L0_attn_in['proj_weight'], 'L0_attn_proj_bias': _L0_attn_in['proj_bias'], 'L0_ffn_gate_w': _L0_ffn_in['gate_w'], 'L0_ffn_expert_w': _L0_ffn_in['expert_w']}

def reference(x, L0_tok_h0, L0_attn_qkv_weight, L0_attn_proj_weight, L0_attn_proj_bias, L0_ffn_gate_w, L0_ffn_expert_w):
    import jax
    import jax.numpy as jnp

    def _L0_tok_ref(x, h0):
        import jax, jax.numpy as jnp
        import numpy as np
        DB4_DEC_LO = np.array([-0.010597401784997278, 0.032883011666982945, 0.030841381835986965, -0.18703481171888114, -0.02798376941698385, 0.6308807679295904, 0.7148465705525415, 0.23037781330885523], dtype=np.float64)
        NUM_LEVELS = 2

        def _afb1d_low(y, h0):
            B, D, N = y.shape
            L = h0.shape[0]
            outsize = (N + L - 1) // 2
            p = 2 * (outsize - 1) - N + L
            yp = jnp.pad(y, ((0, 0), (0, 0), (p // 2, p - p // 2)))
            k = jnp.broadcast_to(h0[None, None, :], (D, 1, L))
            return jax.lax.conv_general_dilated(yp, k, window_strides=(2,), padding='VALID', dimension_numbers=('NCH', 'OIH', 'NCH'), feature_group_count=D)
        y = jnp.swapaxes(x, 1, 2)
        for _ in range(NUM_LEVELS):
            y = _afb1d_low(y, h0)
        return jnp.swapaxes(y, 1, 2)

    def _L0_attn_ref(x, qkv_weight, proj_weight, proj_bias):
        import jax, jax.numpy as jnp
        import numpy as np
        NUM_HEADS = 32
        EPS = 1e-15
        B, N, C = x.shape
        H = NUM_HEADS
        D = C // H
        qkv = jax.nn.relu(jnp.einsum('bnc,oc->bno', x, qkv_weight))
        qkv = qkv.reshape(B, N, 3, H, D)
        q, k, v = (qkv[:, :, 0], qkv[:, :, 1], qkv[:, :, 2])
        v_pad = jnp.concatenate([v, jnp.ones((B, N, H, 1), dtype=v.dtype)], axis=-1)
        vk = jnp.einsum('bnhe,bnhd->bhed', v_pad.astype(jnp.float32), k.astype(jnp.float32))
        vk_q = jnp.einsum('bhed,bnhd->bnhe', vk, q.astype(jnp.float32))
        proj_input = (vk_q[..., :D] / (vk_q[..., D:] + EPS)).astype(qkv.dtype)
        proj_input = proj_input.reshape(B, N, C)
        y = jnp.einsum('bnc,oc->bno', proj_input, proj_weight) + proj_bias
        return y

    def _L0_ffn_ref(x, gate_w, expert_w):
        import jax, jax.numpy as jnp
        import numpy as np
        B, S, H, E = (2, 2048, 256, 8)
        SCALE = 0.5
        scores = jnp.einsum('bsh,eh->bse', x, gate_w)
        chosen = jnp.argmax(scores, axis=-1)
        onehot = jax.nn.one_hot(chosen, gate_w.shape[0], dtype=x.dtype)
        expert_out = jnp.einsum('bsh,efh->bsef', x, expert_w)
        return x + jnp.einsum('bsef,bse->bsf', expert_out, onehot)
    h = _L0_tok_ref(x, L0_tok_h0)
    h = h + _L0_attn_ref(_layernorm(h, axis=-1), L0_attn_qkv_weight, L0_attn_proj_weight, L0_attn_proj_bias)
    h = h + _L0_ffn_ref(_layernorm(h, axis=-1), L0_ffn_gate_w, L0_ffn_expert_w)
    return h

_drawn_inputs = setup_inputs


def setup_inputs(seed=0):
    import zlib

    import numpy as np

    out = dict(_drawn_inputs(seed))
    spreads = {}
    factors = {'L0_attn_proj_bias': 6.347, 'L0_ffn_gate_w': 2.9}
    for name, (base, spread) in spreads.items():
        noise = np.random.default_rng([zlib.crc32(name.encode()), seed]).standard_normal(out[name].shape)
        drawn = base * np.exp(spread * noise) if base else spread * noise
        out[name] = jnp.asarray(drawn.astype(out[name].dtype))
    for name, factor in factors.items():
        out[name] = (out[name] * factor).astype(out[name].dtype)
    return out
```

```python
from contextlib import ExitStack

import concourse.bass as bass
from concourse import mybir

F32 = mybir.dt.float32
ALU = mybir.AluOpType
ACT = mybir.ActivationFunctionType
AX_X = mybir.AxisListType.X

P = 128
C = 256
KC = C // P
TAPS = 8
GRP = 32
HD = 8
E = 8
EPS = 1e-5
DEN_EPS = 1e-15


def audio_tower(nc, x, h0, wqkvT, wprojT, bias, gateT, wexpT, ident_c, mask_c, tap_c, tie_c, out):
    B, N, _ = x.shape
    NL1 = (N + TAPS - 1) // 2
    NT = (NL1 + TAPS - 1) // 2
    NJ = NT // GRP
    NP = B // 2
    TT = 2 * NT // P
    Q = 2 * NJ
    LEAD = 3 * (TAPS - 2)
    SPAN = 4 * (GRP - 1) + 3 * (TAPS - 1) + 1
    EXTRA = SPAN - P
    FIRST = P - EXTRA
    MID = 2 * (GRP - 1) + TAPS
    NG = C // GRP
    HPG = P // HD
    assert NT % GRP == 0 and (2 * NT) % P == 0 and TT == 3 and FIRST == 4 * GRP - LEAD
    assert FIRST + P * (NJ - 1) == N and NT == 3 * 64

    xp = x.rearrange("(s b) n c -> s n b c", b=2)
    outp = out.rearrange("b t c -> (b t) c").rearrange("(s k p) c -> s p k c", p=P, k=TT)

    with ExitStack() as ctx:
        def sb(name, shape, dt=F32):
            return ctx.enter_context(nc.sbuf_tensor(name, shape, dt))

        def sem(name):
            return ctx.enter_context(nc.semaphore(name))

        def two(name, shape, dt=F32):
            return [sb(f"{name}{i}", shape, dt) for i in range(2)]

        wqkv = sb("wqkv", [P, KC, 3 * C])
        wproj = sb("wproj", [P, KC, C])
        gate = sb("gate", [P, KC, E])
        wexp = sb("wexp", [P, KC, E * C])
        bias_bc = sb("bias_bc", [P, C])
        ident = sb("ident", [P, P])
        mask = sb("mask", [P, P + HPG])
        tie = sb("tie", [P, TT * E])
        taps = sb("taps", [MID, TAPS, 2 * P + GRP])
        h0_bc = sb("h0_bc", [MID, TAPS])
        tap_terms = sb("tap_terms", [MID, TAPS, 2 * P + GRP])
        levels = sb("levels", [MID, 2 * P + GRP])
        filt = sb("filt", [P, 3, GRP])
        eps_t = sb("eps_t", [P, 1])
        xb = two("xb", [P, Q, C])
        h = two("h", [P, TT * C])
        hb = two("hb", [P, TT * C])
        stats1, stats2 = two("stats1_", [P, TT, 6]), two("stats2_", [P, TT, 6])
        mv1, mv2 = two("mv1_", [P, TT, 2]), two("mv2_", [P, TT, 2])
        std1, std2 = two("std1_", [P, TT]), two("std2_", [P, TT])
        rstd1, rstd2 = two("rstd1_", [P, TT]), two("rstd2_", [P, TT])
        xn1 = two("xn1_", [P, TT, C])
        xT = two("xT", [P, KC, TT * P])
        kv = two("kv", [P, 4, 2 * NG, GRP + 1])
        qT = two("qT", [P, KC, TT * P])
        bd = two("bd", [P, 2, KC, P + HPG])
        rden = two("rden", [P, TT, 2 * HPG])
        den = two("den", [P, TT, 2 * HPG])
        att = two("att", [P, TT, C])
        attT = two("attT", [P, KC, TT * P])
        h2 = two("h2_", [P, TT * C])
        xn2 = two("xn2_", [P, TT, C])
        x2T = two("x2T", [P, KC, TT * P])
        acc = two("acc", [P, TT, C])
        score = two("score", [P, TT * E])
        smax = two("smax", [P, TT])
        key = two("key", [P, TT * E])
        kmax = two("kmax", [P, TT])
        onehot = two("onehot", [P, TT * E])

        banks = [ctx.enter_context(nc.psum_tensor(f"bank{i}", [P, 2, 512], F32)) for i in range(2)]
        conv_ps, tr_ps = banks
        conv_flat = conv_ps[:, :, :].rearrange("p a b -> p (a b)")
        b4, b5, b6, b7 = [ctx.enter_context(nc.psum_tensor(f"ps{i}", [P, 512], F32)) for i in range(4, 8)]

        x_loaded = [sem("x_loaded0"), sem("x_loaded1")]
        stored = [sem("stored0"), sem("stored1")]
        names = """const_loaded w_loaded kv_ones filt_terms filt_levels filt_ps filt_ready
            conv_done h_ready hb_ready stats1_done var1_ready std1_ready rstd1_ready xn1_ready
            t1_done xT_ready kv_done kv_act kv_dve q_done q0_ready q1_ready vk_done bd_ready
            vkq_done den_copied rden_ready att_ready at_done attT_ready proj_done h2_ready
            stats2_done var2_ready std2_ready rstd2_ready xn2_ready t2_done x2T_ready
            score_done score_copied smax_ready eq_ready key_ready kmax_ready onehot_ready
            r_ready ffn_done acc_half ffn_used""".split()
        S = {n: sem(n) for n in names}

        block = ctx.enter_context(nc.Block())

        def run_steps(eng, step):
            step(-1, 1, 1, now=False, prev=False)
            step(0, 0, 1, prev=False)
            step(1, 1, 2)
            step(2, 0, 2)
            with eng.Fori(1, NP // 2 - 1) as i:
                step(i * 2 + 1, 1, i + 2)
                step(i * 2 + 2, 0, i + 2)
            step(NP - 1, 1, NP // 2 + 1, nxt=False)
            step(NP, 0, NP // 2 + 1, nxt=False, now=False)


        @block.sync
        def _(sp):
            sp.dma_start(taps[:, :, :], tap_c).then_inc(S["const_loaded"], 16)
            sp.dma_start(h0_bc[:, :], h0.rearrange("(a k) -> a k", a=1).to_broadcast([MID, TAPS])).then_inc(S["const_loaded"], 16)

            def load(s, a):
                xs = xp[s]
                sp.dma_start(xb[a][:, 0:Q:NJ, :], xs[0:P, :, :]).then_inc(x_loaded[a], 16)
                for b in range(2):
                    sp.dma_start(xb[a][:, NJ * b + 1:NJ * (b + 1), :],
                                 xs[FIRST:N, b, :].rearrange("(j p) c -> p j c", p=P)).then_inc(x_loaded[a], 16)

            load(0, 0)
            sp.dma_start(ident[:, :], ident_c).then_inc(S["w_loaded"], 16)
            sp.dma_start(mask[:, :], mask_c).then_inc(S["w_loaded"], 16)
            sp.dma_start(tie[:, :], tie_c).then_inc(S["w_loaded"], 16)
            sp.dma_start(bias_bc[:, :], bias.rearrange("(a k) -> a k", a=1).to_broadcast([P, C])).then_inc(S["w_loaded"], 16)
            sp.dma_start(wqkv[:, :, :], wqkvT.rearrange("(k p) o -> p k o", p=P)).then_inc(S["w_loaded"], 16)
            sp.dma_start(wproj[:, :, :], wprojT.rearrange("(k p) o -> p k o", p=P)).then_inc(S["w_loaded"], 16)
            sp.dma_start(gate[:, :, :], gateT.rearrange("(k p) o -> p k o", p=P)).then_inc(S["w_loaded"], 16)
            load(1, 1)
            sp.dma_start(wexp[:, :, :], wexpT.rearrange("(k p) o -> p k o", p=P)).then_inc(S["w_loaded"], 16)

            def step(s, a, now=True, prev=True, nxt=True, more=True):
                if nxt and more:
                    sp.wait_ge(S["conv_done"], s + 2)
                    load(s + 3, 1 - a)
                if prev:
                    sp.wait_ge(S["ffn_used"], 4 * TT * s)
                    sp.dma_start(outp[s - 1], acc[1 - a][:, :, :]).then_inc(stored[1 - a], 16)

            step(-1, 1, now=False, prev=False)
            step(0, 0, prev=False)
            with sp.Fori(0, NP // 2 - 2) as i:
                step(i * 2 + 1, 1)
                step(i * 2 + 2, 0)
            step(NP - 3, 1, more=False)
            step(NP - 2, 0, more=False)
            step(NP - 1, 1, nxt=False)
            step(NP, 0, nxt=False, now=False)
            for a in range(2):
                sp.wait_ge(stored[a], 16 * NP // 2)

        @block.gpsimd
        def _(pool):
            for a in range(2):
                nc.gpsimd.memset(kv[a][:, :, :, :], 0.0).then_inc(S["kv_ones"], 1)
            pool.wait_ge(S["kv_ones"], 2)
            for a in range(2):
                nc.gpsimd.memset(kv[a][:, :, NG:, GRP:], 1.0).then_inc(S["kv_ones"], 1)
            pool.wait_ge(S["w_loaded"], 8 * 16)

            def step(s, a, turn, now=True, prev=True, nxt=True):
                if prev:
                    pool.wait_ge(S["xn2_ready"], TT * s)
                    if not (isinstance(s, int) and s < 3):
                        pool.wait_ge(stored[1 - a], 16 * (turn - 2))
                    nc.gpsimd.tensor_tensor(acc[1 - a][:, :, :], h2[1 - a][:, :].rearrange("p (k c) -> p k c", c=C),
                                            xn2[1 - a][:, :, :], ALU.add).then_inc(S["r_ready"], 1)
                if nxt:
                    pool.wait_ge(S["h_ready"], s + 2)
                    if prev:
                        pool.wait_ge(S["h2_ready"], s)
                    for t in range(TT):
                        ins = nc.gpsimd.tensor_tensor(hb[1 - a][:, t * C:(t + 1) * C], h[1 - a][:, t * C:(t + 1) * C],
                                                      bias_bc[:, :], ALU.add)
                    ins.then_inc(S["hb_ready"], 1)

            run_steps(pool, step)

        @block.scalar
        def _(act):
            act.wait_ge(S["filt_ps"], 1)
            nc.scalar.activation(filt[:, :, :], b4[:, 0:3 * GRP].rearrange("p (m o) -> p m o", o=GRP), ACT.Copy).then_inc(S["filt_ready"], 1)

            def step(s, a, turn, now=True, prev=True, nxt=True):
                n = 1 - a
                if now:
                    act.wait_ge(S["kv_ones"], 4)
                    act.wait_ge(S["kv_done"], TT * s + 1)
                    nc.scalar.activation(kv[a][:, 0, :, 0:GRP], b5[:, :].rearrange("p (g c) -> p g c", c=GRP), ACT.Relu).then_inc(S["kv_act"], 1)
                    act.wait_ge(S["kv_done"], TT * s + 3)
                    nc.scalar.activation(kv[a][:, 3, :, 0:GRP], b7[:, :].rearrange("p (g c) -> p g c", c=GRP), ACT.Relu).then_inc(S["kv_act"], 1)
                    act.wait_ge(S["q_done"], KC * s + 2)
                    nc.scalar.activation(qT[a][:, 1, :], b5[:, 0:TT * P], ACT.Relu).then_inc(S["q1_ready"], 1)
                if prev:
                    act.wait_ge(S["var2_ready"], s)
                    nc.scalar.activation(std2[n][:, :], mv2[n][:, :, 1], ACT.Sqrt, bias=eps_t[:, 0:1]).then_inc(S["std2_ready"], 1)
                if nxt:
                    act.wait_ge(S["conv_done"], s + 2)
                    if prev:
                        act.wait_ge(S["hb_ready"], s)
                    nc.scalar.activation(h[n][:, :], conv_flat[:, 0:TT * C], ACT.Copy).then_inc(S["h_ready"], 1)
                    act.wait_ge(S["var1_ready"], s + 2)
                    nc.scalar.activation(std1[n][:, :], mv1[n][:, :, 1], ACT.Sqrt, bias=eps_t[:, 0:1]).then_inc(S["std1_ready"], 1)
                    act.wait_ge(S["t1_done"], s + 2)
                    if prev:
                        act.wait_ge(S["q_done"], KC * s)
                    nc.scalar.activation(xT[n][:, :, :], tr_ps[:, :, 0:TT * P], ACT.Copy).then_inc(S["xT_ready"], 1)
                if prev:
                    act.wait_ge(S["t2_done"], s)
                    nc.scalar.activation(x2T[n][:, :, :], conv_ps[:, :, 0:TT * P], ACT.Copy).then_inc(S["x2T_ready"], 1)
                if now:
                    for m, bank in enumerate((b4, b5)):
                        act.wait_ge(S["at_done"], KC * s + m + 1)
                        nc.scalar.activation(attT[a][:, m, :], bank[:, 0:TT * P], ACT.Copy).then_inc(S["attT_ready"], 1)

            run_steps(act, step)

        @block.vector
        def _(dve):
            nc.vector.memset(eps_t[:, :], EPS)
            dve.wait_ge(S["const_loaded"], 32)
            for k in range(TAPS):
                nc.vector.tensor_scalar(tap_terms[:, k, :], taps[:, k, :], h0_bc[:, k:k + 1], None, ALU.mult).then_inc(S["filt_terms"], 1)
            dve.wait_ge(S["filt_terms"], TAPS)
            nc.vector.tensor_reduce(levels[:, :], tap_terms[:, :, :].rearrange("p k x -> p x k"), AX_X, ALU.add).then_inc(S["filt_levels"], 1)
            dve.wait_ge(S["w_loaded"], 8 * 16)

            def norm(src, dst, st, mv, std, rstd, cnt, stats_done, var_ready, std_ready, rstd_ready, ready):
                for t in range(TT):
                    nc.vector.bn_stats(st[:, t, :], src[:, t * C:(t + 1) * C]).then_inc(S[stats_done], 1)
                dve.wait_ge(S[stats_done], TT * cnt)
                dve.nop(nofuse=True)
                for t in range(TT):
                    ins = nc.vector.bn_aggr(mv[:, t, :], st[:, t, :])
                ins.then_inc(S[var_ready], 1)
                dve.wait_ge(S[std_ready], cnt)
                nc.vector.reciprocal(rstd[:, :], std[:, :]).then_inc(S[rstd_ready], 1)
                dve.wait_ge(S[rstd_ready], cnt)
                for t in range(TT):
                    nc.vector.tensor_scalar(dst[:, t, :], src[:, t * C:(t + 1) * C], mv[:, t, 0:1], rstd[:, t:t + 1],
                                            ALU.subtract, ALU.mult).then_inc(S[ready], 1)

            def step(s, a, turn, now=True, prev=True, nxt=True):
                n = 1 - a
                if now:
                    dve.wait_ge(S["kv_ones"], 4)
                    dve.wait_ge(S["kv_done"], TT * s + 2)
                    nc.vector.tensor_scalar_max(kv[a][0:64, 1, :, 0:GRP], b6[0:64, :].rearrange("p (g c) -> p g c", c=GRP), 0.0)
                    nc.vector.tensor_scalar_max(kv[a][64:P, 2, :, 0:GRP], b6[64:P, :].rearrange("p (g c) -> p g c", c=GRP), 0.0).then_inc(S["kv_dve"], 1)
                    dve.wait_ge(S["q_done"], KC * s + 1)
                    nc.vector.tensor_scalar_max(qT[a][:, 0, :], b4[:, 0:TT * P], 0.0).then_inc(S["q0_ready"], 1)
                if prev:
                    dve.wait_ge(S["proj_done"], s)
                    dve.wait_ge(S["hb_ready"], s)
                    nc.vector.tensor_tensor(h2[n][:, 0:2 * C], b6[:, :], hb[n][:, 0:2 * C], ALU.add)
                    nc.vector.tensor_tensor(h2[n][:, 2 * C:3 * C], b7[:, 0:C], hb[n][:, 2 * C:3 * C], ALU.add).then_inc(S["h2_ready"], 1)
                    dve.wait_ge(S["h2_ready"], s)
                    norm(h2[n], xn2[n], stats2[n], mv2[n], std2[n], rstd2[n], s,
                         "stats2_done", "var2_ready", "std2_ready", "rstd2_ready", "xn2_ready")
                if now:
                    dve.wait_ge(S["vk_done"], s + 1)
                    if prev:
                        dve.wait_ge(S["vkq_done"], TT * s)
                    vk = b4[:, 0:4 * (GRP + 1)].rearrange("p (m e) -> p m e", e=GRP + 1)
                    for b in range(2):
                        for m in range(KC):
                            i = KC * b + m
                            nc.vector.tensor_tensor(bd[a][:, b, m, 0:P].rearrange("p (g e) -> p g e", e=GRP),
                                                    vk[:, i:i + 1, 0:GRP].to_broadcast([P, P // GRP, GRP]),
                                                    mask[:, 0:P].rearrange("p (g e) -> p g e", e=GRP), ALU.mult)
                    for b in range(2):
                        for m in range(KC):
                            i = KC * b + m
                            ins = nc.vector.tensor_scalar(bd[a][:, b, m, P:], mask[:, P:], vk[:, i, GRP:GRP + 1], None, ALU.mult)
                    ins.then_inc(S["bd_ready"], 1)
                if nxt:
                    dve.wait_ge(S["h_ready"], s + 2)
                    norm(h[n], xn1[n], stats1[n], mv1[n], std1[n], rstd1[n], s + 2,
                         "stats1_done", "var1_ready", "std1_ready", "rstd1_ready", "xn1_ready")
                if now:
                    for t, bank in enumerate((b5, b6, b7)):
                        nd = bank[:, 0:KC * (P + HPG)].rearrange("p (m e) -> p m e", e=P + HPG)
                        dve.wait_ge(S["vkq_done"], TT * s + t + 1)
                        nc.vector.tensor_scalar_add(den[a][:, t, :].rearrange("p (m e) -> p m e", e=HPG), nd[:, :, P:], DEN_EPS).then_inc(S["den_copied"], 1)
                        dve.wait_ge(S["den_copied"], TT * s + t + 1)
                        nc.vector.reciprocal(rden[a][:, t, :], den[a][:, t, :]).then_inc(S["rden_ready"], 1)
                        dve.wait_ge(S["rden_ready"], TT * s + t + 1)
                        for m in range(KC):
                            ins = nc.vector.tensor_tensor(
                                att[a][:, t, m * P:(m + 1) * P].rearrange("p (g e) -> p g e", e=HD),
                                nd[:, m, 0:P].rearrange("p (g e) -> p g e", e=HD),
                                rden[a][:, t, m * HPG:(m + 1) * HPG].rearrange("p (g o) -> p g o", o=1).to_broadcast([P, HPG, HD]),
                                ALU.mult)
                        ins.then_inc(S["att_ready"], 1)
                if prev:
                    sc3 = score[n][:, :].rearrange("p (t e) -> p t e", e=E)
                    k3 = key[n][:, :].rearrange("p (t e) -> p t e", e=E)
                    o3 = onehot[n][:, :].rearrange("p (t e) -> p t e", e=E)

                    def spread(v):
                        return v[:, :].rearrange("p (t o) -> p t o", o=1).to_broadcast([P, TT, E])
                    dve.wait_ge(S["score_done"], s)
                    nc.vector.tensor_copy(score[n][:, :], b6[:, 0:TT * E]).then_inc(S["score_copied"], 1)
                    dve.wait_ge(S["score_copied"], s)
                    nc.vector.tensor_reduce(smax[n][:, :], sc3, AX_X, ALU.max).then_inc(S["smax_ready"], 1)
                    dve.wait_ge(S["smax_ready"], s)
                    nc.vector.tensor_tensor(k3, sc3, spread(smax[n]), ALU.is_equal).then_inc(S["eq_ready"], 1)
                    dve.wait_ge(S["eq_ready"], s)
                    nc.vector.tensor_tensor(key[n][:, :], key[n][:, :], tie[:, :], ALU.mult).then_inc(S["key_ready"], 1)
                    dve.wait_ge(S["key_ready"], s)
                    nc.vector.tensor_reduce(kmax[n][:, :], k3, AX_X, ALU.max).then_inc(S["kmax_ready"], 1)
                    dve.wait_ge(S["kmax_ready"], s)
                    nc.vector.tensor_tensor(o3, k3, spread(kmax[n]), ALU.is_equal).then_inc(S["onehot_ready"], 1)
                    dve.wait_ge(S["onehot_ready"], s)
                    dve.wait_ge(S["r_ready"], s)
                    c = 0
                    for t in range(TT):
                        for e2 in range(E // 2):
                            bank = (b6, b7)[c % 2]
                            dve.wait_ge(S["ffn_done"], 4 * TT * (s - 1) + c + 1)
                            for j in range(2):
                                e = 2 * e2 + j
                                ins = nc.vector.scalar_tensor_tensor(
                                    acc[n][:, t, :], bank[:, j * C:(j + 1) * C], onehot[n][:, t * E + e:t * E + e + 1],
                                    acc[n][:, t, :], ALU.mult, ALU.add)
                                if j == 0:
                                    ins.then_inc(S["acc_half"], 1)
                                    dve.wait_ge(S["acc_half"], 4 * TT * (s - 1) + c + 1)
                            ins.then_inc(S["ffn_used"], 1)
                            dve.wait_ge(S["ffn_used"], 4 * TT * (s - 1) + c + 1)
                            c += 1

            run_steps(dve, step)

        @block.tensor
        def _(pe):
            pe.wait_ge(S["filt_levels"], 1)
            second = levels[:, 2 * P:]
            nc.tensor.matmul(b4[:, 0:GRP], levels[:, LEAD:LEAD + P], second, start=True, stop=True)
            nc.tensor.matmul(b4[:, GRP:2 * GRP], levels[:, 0:P], second, start=True, stop=True)
            nc.tensor.matmul(b4[:, 2 * GRP:3 * GRP], levels[:, P:2 * P], second, start=True, stop=True).then_inc(S["filt_ps"], 1)
            pe.wait_ge(S["filt_ready"], 1)

            def conv(a, x_count):
                pe.wait_ge(x_loaded[a], x_count)
                for t in range(TT):
                    for g in range(4):
                        q = 4 * t + g
                        ins = nc.tensor.matmul(conv_flat[GRP * g:GRP * (g + 1), t * C:(t + 1) * C],
                                               filt[:, 0 if q % NJ == 0 else 1, :], xb[a][:, q, :],
                                               start=True, stop=q % NJ in (0, NJ - 1), tile_position=(0, GRP * g))
                    for g in range(4):
                        q = 4 * t + g
                        if q % NJ not in (0, NJ - 1):
                            ins = nc.tensor.matmul(conv_flat[GRP * g:GRP * (g + 1), t * C:(t + 1) * C],
                                                   filt[:, 2, :], xb[a][:, q + 1, :],
                                                   start=False, stop=True, tile_position=(0, GRP * g))
                ins.then_inc(S["conv_done"], 1)

            def flip(dst, src, s_ready, base):
                for t in range(TT):
                    pe.wait_ge(S[s_ready], base + t + 1)
                    for m in range(KC):
                        ins = nc.tensor.transpose(dst(m)[:, t * P:(t + 1) * P], src[:, t, m * P:(m + 1) * P], ident[:, :])
                return ins

            def step(s, a, turn, now=True, prev=True, nxt=True):
                n = 1 - a
                if now:
                    pe.wait_ge(S["xT_ready"], s + 1)
                    if prev:
                        pe.wait_ge(S["attT_ready"], KC * s)
                    for t, bank in enumerate((b5, b6, b7)):
                        if prev and t == 1:
                            pe.wait_ge(S["ffn_used"], 4 * TT * (s - 1))
                        for k in range(KC):
                            ins = nc.tensor.matmul(bank[:, :], xT[a][:, k, t * P:(t + 1) * P], wqkv[:, k, C:],
                                                   start=k == 0, stop=k == KC - 1)
                        ins.then_inc(S["kv_done"], 1)
                    for m, bank in enumerate((b4, b5)):
                        if m == 1:
                            pe.wait_ge(S["kv_act"], 2 * s + 1)
                        for k in range(KC):
                            ins = nc.tensor.matmul(bank[:, 0:TT * P], wqkv[:, k, m * P:(m + 1) * P], xT[a][:, k, :],
                                                   start=k == 0, stop=k == KC - 1)
                        ins.then_inc(S["q_done"], 1)
                if prev:
                    pe.wait_ge(S["attT_ready"], KC * s)
                    if now:
                        pe.wait_ge(S["kv_dve"], s + 1)
                        pe.wait_ge(S["kv_act"], 2 * s + 2)
                    else:
                        pe.wait_ge(S["ffn_used"], 4 * TT * (s - 1))
                    for t in range(TT):
                        o = b6[:, t * C:(t + 1) * C] if t < 2 else b7[:, 0:C]
                        for k in range(KC):
                            ins = nc.tensor.matmul(o, attT[n][:, k, t * P:(t + 1) * P], wproj[:, k, :],
                                                   start=k == 0, stop=k == KC - 1)
                    ins.then_inc(S["proj_done"], 1)
                if nxt:
                    if prev and not (isinstance(s, int) and s < 2):
                        pe.wait_ge(S["x2T_ready"], s - 1)
                    conv(n, 48 * turn)
                if now:
                    pe.wait_ge(S["kv_act"], 2 * s + 2)
                    pe.wait_ge(S["kv_dve"], s + 1)
                    pe.wait_ge(S["q0_ready"], s + 1)
                    for b in range(2):
                        for m in range(KC):
                            i = KC * b + m
                            for k, seg in enumerate(((0, 1), (3, 2))[b]):
                                for g in range(4):
                                    ins = nc.tensor.matmul(b4[GRP * g:GRP * (g + 1), i * (GRP + 1):(i + 1) * (GRP + 1)],
                                                           kv[a][:, seg, 4 * m + g, 0:GRP], kv[a][:, seg, NG + 4 * m + g, :],
                                                           start=k == 0, stop=k == 1, tile_position=(0, GRP * g))
                    ins.then_inc(S["vk_done"], 1)
                if nxt:
                    flip(lambda m: tr_ps[:, m, :], xn1[n], "xn1_ready", TT * (s + 1)).then_inc(S["t1_done"], 1)
                if now:
                    pe.wait_ge(S["bd_ready"], s + 1)
                    pe.wait_ge(S["q1_ready"], s + 1)
                    if prev:
                        pe.wait_ge(S["h2_ready"], s)
                    for t, bank in enumerate((b5, b6, b7)):
                        for m in range(KC):
                            o = bank[:, m * (P + HPG):(m + 1) * (P + HPG)]
                            if t == 1:
                                for b in range(2):
                                    ins = nc.tensor.matmul(o[64 * b:64 * b + 64, :], qT[a][:, m, P + 64 * b:P + 64 * b + 64],
                                                           bd[a][:, b, m, :], start=True, stop=True, tile_position=(0, 64 * b))
                            else:
                                ins = nc.tensor.matmul(o, qT[a][:, m, t * P:(t + 1) * P], bd[a][:, t // 2, m, :],
                                                       start=True, stop=True)
                        ins.then_inc(S["vkq_done"], 1)
                if prev:
                    if nxt:
                        pe.wait_ge(S["h_ready"], s + 2)
                    flip(lambda m: conv_ps[:, m, :], xn2[n], "xn2_ready", TT * (s - 1)).then_inc(S["t2_done"], 1)
                if now:
                    for m, bank in enumerate((b4, b5)):
                        pe.wait_ge(S["att_ready"], TT * s + TT)
                        for t in range(TT):
                            ins = nc.tensor.transpose(bank[:, t * P:(t + 1) * P], att[a][:, t, m * P:(m + 1) * P], ident[:, :])
                        ins.then_inc(S["at_done"], 1)
                if prev:
                    pe.wait_ge(S["x2T_ready"], s)
                    if now:
                        pe.wait_ge(S["att_ready"], TT * s + TT)
                    else:
                        pe.wait_ge(S["h2_ready"], s)
                    for t in range(TT):
                        for k in range(KC):
                            ins = nc.tensor.matmul(b6[:, t * E:(t + 1) * E], x2T[n][:, k, t * P:(t + 1) * P], gate[:, k, :],
                                                   start=k == 0, stop=k == KC - 1)
                    ins.then_inc(S["score_done"], 1)
                    pe.wait_ge(S["score_copied"], s)
                    c = 0
                    for t in range(TT):
                        for e2 in range(E // 2):
                            bank = (b6, b7)[c % 2]
                            if c >= 2:
                                pe.wait_ge(S["ffn_used"], 4 * TT * (s - 1) + c - 1)
                            for k in range(KC):
                                ins = nc.tensor.matmul(bank[:, :], x2T[n][:, k, t * P:(t + 1) * P],
                                                       wexp[:, k, 2 * e2 * C:2 * (e2 + 1) * C], start=k == 0, stop=k == KC - 1)
                            ins.then_inc(S["ffn_done"], 1)
                            c += 1

            pe.wait_ge(S["w_loaded"], 8 * 16)
            run_steps(pe, step)


_INS = ['x', 'L0_tok_h0', 'L0_attn_qkv_weight', 'L0_attn_proj_weight', 'L0_attn_proj_bias', 'L0_ffn_gate_w', 'L0_ffn_expert_w']
_OUTS = [((16, 192, 256), 'float32')]


def kernel(**inputs):
    import numpy as _np
    import concourse.bacc as _bacc
    from concourse import mybir as _mybir
    from concourse.bass_utils import run_bass_kernel_spmd as _run

    put = {
        "x": inputs["x"],
        "h0": inputs["L0_tok_h0"],
        "wqkvT": _np.transpose(inputs["L0_attn_qkv_weight"]),
        "wprojT": _np.transpose(inputs["L0_attn_proj_weight"]),
        "bias": inputs["L0_attn_proj_bias"],
        "gateT": _np.transpose(inputs["L0_ffn_gate_w"]),
        "wexpT": _np.transpose(inputs["L0_ffn_expert_w"], (2, 0, 1)).reshape(C, E * C),
    }
    put["ident_c"] = _np.eye(P, dtype=_np.float32)
    row = _np.arange(P)[:, None]
    put["mask_c"] = _np.concatenate([row // HD == _np.arange(P)[None, :] // HD,
                                     row // HD == _np.arange(P // HD)[None, :]], axis=1).astype(_np.float32)
    mid = _np.arange(2 * (GRP - 1) + TAPS)[:, None, None]
    tap = _np.arange(TAPS)[None, :, None]
    put["tap_c"] = _np.concatenate([_np.arange(2 * P)[None, None, :] - 2 * mid == tap,
                                    mid - 2 * _np.arange(GRP)[None, None, :] == tap], axis=2).astype(_np.float32)
    put["tie_c"] = _np.tile(_np.arange(E, 0, -1, dtype=_np.float32), (P, 3))

    nc = _bacc.Bacc("TRN2", target_bir_lowering=False, num_devices=1)
    arrays, args = {}, []
    for name, a in put.items():
        a = _np.ascontiguousarray(a)
        arrays[f"in_{name}_dram"] = a
        args.append(nc.dram_tensor(f"in_{name}_dram", a.shape, _mybir.dt.from_np(a.dtype), kind="ExternalInput").ap())
    for i, (shape, dtype) in enumerate(_OUTS):
        dt = _mybir.dt.from_np(_np.dtype(dtype))
        args.append(nc.dram_tensor(f"out_{i}_dram", shape, dt, kind="ExternalOutput").ap())
    audio_tower(nc, *args)
    r = _run(nc, [arrays], core_ids=[0])
    return r.results[0]["out_0_dram"]
```

```python
from contextlib import ExitStack

import concourse.bass as bass
from concourse import mybir

F32 = mybir.dt.float32
F32R = mybir.dt.float32r
BF16 = mybir.dt.bfloat16
I32 = mybir.dt.int32
U32 = mybir.dt.uint32
ALU = mybir.AluOpType
ACT = mybir.ActivationFunctionType
AX_X = mybir.AxisListType.X

P = 128
C = 256
KC = C // P
TAPS = 8
GRP = 32
HD = 8
E = 8
EPS = 1e-5
DEN_EPS = 1e-15


TILES = 3072 // P + E - 1
REGION = 3072 + P
BIG = 1 << 20
RSTD, SHIFT, TOKEN = C, C + 1, C + 2
ROW = C + 3
RING = 8

CONSTS = {}
_at = 0
for _name, _width in (("ident", P), ("mask", P + P // HD), ("tie", 3 * E), ("ids", 2 * 3), ("start", E), ("before", P),
                      ("full", 3072 // P), ("upto", E * E), ("tile", TILES), ("rows", TILES), ("base", E), ("lane", 1)):
    CONSTS[_name] = (_at, _at + _width)
    _at += _width
NCONST = _at


def audio_tower(nc, x, h0, wqkvT, wprojT, bias, gateT, wexpT, const_c, tap_c, out):
    B, N, _ = x.shape
    NL1 = (N + TAPS - 1) // 2
    NT = (NL1 + TAPS - 1) // 2
    NJ = NT // GRP
    NP = B // 2
    TT = 2 * NT // P
    Q = 2 * NJ
    LEAD = 3 * (TAPS - 2)
    SPAN = 4 * (GRP - 1) + 3 * (TAPS - 1) + 1
    EXTRA = SPAN - P
    FIRST = P - EXTRA
    MID = 2 * (GRP - 1) + TAPS
    RANK = 448
    NG = C // GRP
    HPG = P // HD
    assert NT % GRP == 0 and (2 * NT) % P == 0 and TT == 3 and FIRST == 4 * GRP - LEAD
    assert FIRST + P * (NJ - 1) == N and NT == 3 * 64

    xp = x.rearrange("(s b) n c -> s n b c", b=2)
    out_rows = out.rearrange("b t c -> (b t) c")
    NTOK = B * NT
    assert NTOK == 3072
    sorted_rows = nc.dram_tensor("sorted_rows", (E * REGION, ROW), F32, kind="Internal").ap()

    with ExitStack() as ctx:
        def sb(name, shape, dt=F32):
            return ctx.enter_context(nc.sbuf_tensor(name, shape, dt))

        def sem(name):
            return ctx.enter_context(nc.semaphore(name))

        def two(name, shape, dt=F32):
            return [sb(f"{name}{i}", shape, dt) for i in range(2)]

        gate = sb("gate", [P, KC, E])
        wqkv_hi, wqkv_lo = sb("wqkv_hi", [P, KC, 3 * C], F32R), sb("wqkv_lo", [P, KC, 3 * C], F32R)
        wproj_hi, wproj_lo = sb("wproj_hi", [P, KC, C], F32R), sb("wproj_lo", [P, KC, C], F32R)
        wexp_hi, wexp_lo = sb("wexp_hi", [P, KC, E * C], F32R), sb("wexp_lo", [P, KC, E * C], F32R)
        bias_bc = sb("bias_bc", [P, C])
        consts = sb("consts", [P, NCONST])

        def const(name):
            return consts[:, CONSTS[name][0]:CONSTS[name][1]]

        ident = const("ident")
        mask = const("mask")
        taps = sb("taps", [MID, SPAN + GRP])
        h0_bc = sb("h0_bc", [MID, TAPS])
        stage = sb("stage", [P, E * C])
        tap_terms = stage[0:MID, 0:TAPS * (SPAN + GRP)].rearrange("p (k x) -> p k x", k=TAPS)
        wexp = stage[:, :]
        levels = sb("levels", [MID, 2 * P])
        second = sb("second", [MID, GRP])
        filt = sb("filt", [P, 3, GRP])
        eps_t = sb("eps_t", [P, 1])
        zero_row = sb("zero_row", [P, ROW])
        before = sb("before", [P, P], BF16)
        ones = sb("ones", [P, P], BF16)
        xb = two("xb", [P, Q, C])
        h = two("h", [P, TT * C])
        hb = two("hb", [P, TT * C])
        stats1, stats2 = two("stats1_", [P, TT, 6]), two("stats2_", [P, TT, 6])
        mv1, mv2 = two("mv1_", [P, TT, 2]), two("mv2_", [P, TT, 2])
        std1, std2 = two("std1_", [P, TT]), two("std2_", [P, TT])
        rstd1, shift1 = two("rstd1_", [P, TT]), two("shift1_", [P, TT])
        xn1 = two("xn1_", [P, TT, C])
        xT_hi, xT_lo = two("xT_hi", [P, KC, TT * P], F32R), two("xT_lo", [P, KC, TT * P], F32R)
        kv = two("kv", [P, 4, 2 * NG, GRP + 1])
        qT = two("qT", [P, KC, TT * P])
        bd = two("bd", [P, 2, KC, P + HPG])
        rden = two("rden", [P, TT, 2 * HPG])
        den = two("den", [P, TT, 2 * HPG])
        att = two("att", [P, TT, C])
        attT_hi, attT_lo = two("attT_hi", [P, KC, TT * P], F32R), two("attT_lo", [P, KC, TT * P], F32R)
        row = two("row", [P, TT, ROW])
        xn2 = two("xn2_", [P, TT, C])
        x2T = two("x2T", [P, KC, TT * P])
        wqkv = [xn2[k][:, :, :].rearrange("p t c -> p (t c)") for k in range(KC)]
        wproj = att[1][:, 0:KC, :]
        score = two("score", [P, TT * E])
        smax = two("smax", [P, TT])
        key = two("key", [P, TT * E])
        kmax = two("kmax", [P, TT])
        onehot = two("onehot", [P, TT * E], BF16)
        seen = two("seen", [P, TT, E], BF16)
        place = two("place", [P, TT * E])
        pos_sum = two("pos_sum", [P, TT])
        pos = two("pos", [P, TT], U32)
        count, full_tiles, ends, starts = (sb(n, [P, E]) for n in ("count", "full_tiles", "ends", "starts"))
        first_row, last_row = sb("first_row", [P, E]), sb("last_row", [P, E])
        more = sb("more", [P, E, NTOK // P])
        upto = sb("upto", [P, E, E])
        past = sb("past", [P, TILES, E + 1])
        own = sb("own", [P, TILES, E])
        own_first, own_last = sb("own_first", [P, TILES, E]), sb("own_last", [P, TILES, E])
        expert, row_at, row_end, row_from, twice = (sb(n, [P, TILES]) for n in ("expert", "row_at", "row_end", "row_from", "twice"))
        w_off, r_off = sb("w_off", [P, TILES], I32), sb("r_off", [P, TILES], I32)
        skip = sb("skip", [P, TILES])
        srow = [xb[0][:, :, :].rearrange("p q c -> p (q c)")[:, ROW * i:ROW * (i + 1)] for i in range(RING)]
        y = [xb[1][:, i, :] for i in range(RING)]
        token = [sb(f"token{i}", [P, 1], U32) for i in range(RING)]
        sxn = [xn1[i % 2][:, i // 2, :] for i in range(4)]
        sT_hi = [xT_hi[i % 2][:, :, P * (i // 2):P * (i // 2 + 1)] for i in range(4)]
        sT_lo = [xT_lo[i % 2][:, :, P * (i // 2):P * (i // 2 + 1)] for i in range(4)]

        banks = [ctx.enter_context(nc.psum_tensor(f"bank{i}", [P, 2, 512], F32)) for i in range(2)]
        conv_ps, tr_ps = banks
        conv_flat = conv_ps[:, :, :].rearrange("p a b -> p (a b)")
        b4, b5, b6, b7 = [ctx.enter_context(nc.psum_tensor(f"ps{i}", [P, 512], F32)) for i in range(4, 8)]

        x_loaded = [sem("x_loaded0"), sem("x_loaded1")]
        scattered = [sem("scattered0"), sem("scattered1")]
        srow_loaded = [sem(f"srow_loaded{i}") for i in range(RING)]
        y_stored = [sem(f"y_stored{i}") for i in range(RING)]
        names = """taps_loaded const_loaded w_loaded wexp_loaded margin_stored zero_ready id_start
            kv_ones levels_zero filt_terms filt_levels filt_ps filt_ready w_hi w_split wexp_plus wexp_hi_ready wexp_split rank_consts
            conv_done h_ready hb_ready stats1_done var1_ready std1_ready rstd1_ready shift1_ready xn1_ready
            t1_done xT_hi_ready xT_lo_ready kv_done kv_ready q_done q0_ready q1_ready vk_done bd_ready
            vkq_done den_copied rden_ready att_ready at_done attT_hi_ready attT_lo_ready proj_done h2_ready
            stats2_done var2_ready std2_ready rstd2_ready shift2_ready xn2_ready t2_done x2T_ready
            score_done score_copied smax_ready eq_ready key_ready kmax_ready onehot_ready
            seen_ready rank_done place_ready pos_summed pos_ready id_ready total_done plan_step plan_ready
            sxn_ready st_done sT_hi_ready sT_lo_ready expert_done y_ready""".split()
        S = {n: sem(n) for n in names}

        block = ctx.enter_context(nc.Block())

        def run_steps(eng, step):
            step(-1, 1, 1, now=False, prev=False, old=False)
            step(0, 0, 1, prev=False, old=False)
            step(1, 1, 2, old=False)
            step(2, 0, 2)
            with eng.Fori(1, NP // 2 - 1) as i:
                step(i * 2 + 1, 1, i + 2)
                step(i * 2 + 2, 0, i + 2)
            step(NP - 1, 1, NP // 2 + 1, nxt=False)
            step(NP, 0, NP // 2 + 1, nxt=False, now=False)
            step(NP + 1, 1, NP // 2 + 2, nxt=False, now=False, prev=False)

        def run_tiles(eng, tile):
            for j in range(-4, RING):
                tile(j, j % RING, j // RING)
            with eng.Fori(1, (TILES - 4) // RING) as i:
                for u in range(RING):
                    tile(i * RING + u, u, i)
            for j in range((TILES - 4) // RING * RING, TILES):
                tile(j, j % RING, j // RING)

        def there(k):
            return not isinstance(k, int) or 0 <= k < TILES


        @block.sync
        def _(sp):
            sp.dma_start(taps[:, :], tap_c).then_inc(S["taps_loaded"], 16)
            sp.dma_start(h0_bc[:, :], h0.rearrange("(a k) -> a k", a=1).to_broadcast([MID, TAPS])).then_inc(S["taps_loaded"], 16)

            def load(s, a):
                xs = xp[s]
                sp.dma_start(xb[a][:, 0:Q:NJ, :], xs[0:P, :, :]).then_inc(x_loaded[a], 16)
                for b in range(2):
                    sp.dma_start(xb[a][:, NJ * b + 1:NJ * (b + 1), :],
                                 xs[FIRST:N, b, :].rearrange("(j p) c -> p j c", p=P)).then_inc(x_loaded[a], 16)

            load(0, 0)
            sp.dma_start(consts[:, :], const_c).then_inc(S["const_loaded"], 16)
            sp.dma_start(bias_bc[:, :], bias.rearrange("(a k) -> a k", a=1).to_broadcast([P, C])).then_inc(S["const_loaded"], 16)
            for k in range(KC):
                sp.dma_start(wqkv[k], wqkvT[k * P:(k + 1) * P, :]).then_inc(S["w_loaded"], 16)
            sp.dma_start(wproj, wprojT.rearrange("(k p) o -> p k o", p=P)).then_inc(S["w_loaded"], 16)
            sp.dma_start(gate[:, :, :], gateT.rearrange("(k p) o -> p k o", p=P)).then_inc(S["w_loaded"], 16)
            load(1, 1)
            sp.wait_ge(S["filt_levels"], 1)
            sp.dma_start(wexp, wexpT[0:P, :]).then_inc(S["wexp_loaded"], 16)
            sp.wait_ge(S["zero_ready"], 1)
            margins = sorted_rows.rearrange("(e r) c -> r e c", r=REGION)[0:P, :, :]
            sp.dma_start(margins, zero_row[:, :].rearrange("p (a c) -> p a c", a=1).to_broadcast([P, E, ROW])).then_inc(S["margin_stored"], 16)

            def step(s, a):
                sp.wait_ge(S["conv_done"], s + 2)
                load(s + 3, 1 - a)

            step(-1, 1)
            step(0, 0)
            sp.wait_ge(S["wexp_split"], 1)
            sp.dma_start(wexp, wexpT[P:, :]).then_inc(S["wexp_loaded"], 16)
            with sp.Fori(0, NP // 2 - 2) as i:
                step(i * 2 + 1, 1)
                step(i * 2 + 2, 0)

            sp.wait_ge(S["plan_ready"], 1)
            sp.wait_ge(S["margin_stored"], 16)
            for a in range(2):
                sp.wait_ge(scattered[a], 16 * TT * NP // 2)

            def load_rows(k, u, read_before):
                if read_before:
                    sp.wait_ge(S["y_ready"], k - (RING - 1))
                start = sp.value_load(r_off[0:1, bass.ds(k, 1)], min_val=0, max_val=(E - 1) * REGION + NTOK)
                sp.dma_start(srow[u], sorted_rows[bass.ds(start, P), :]).then_inc(srow_loaded[u], 16)

            for k in range(RING):
                load_rows(k, k, False)
            with sp.Fori(1, TILES // RING) as i:
                for u in range(RING):
                    load_rows(i * RING + u, u, True)
            for k in range(TILES // RING * RING, TILES):
                load_rows(k, k % RING, True)

            for u in range(RING):
                sp.wait_ge(y_stored[u], 16 * ((TILES - u + RING - 1) // RING))

        @block.gpsimd
        def _(pool):
            nc.gpsimd.memset(levels[:, :], 0.0).then_inc(S["levels_zero"], 1)
            nc.gpsimd.memset(zero_row[:, :], 0.0).then_inc(S["zero_ready"], 1)
            for a in range(2):
                nc.gpsimd.memset(kv[a][:, :, :, :], 0.0).then_inc(S["kv_ones"], 1)
            pool.wait_ge(S["kv_ones"], 2)
            for a in range(2):
                nc.gpsimd.memset(kv[a][:, :, NG:, GRP:], 1.0).then_inc(S["kv_ones"], 1)
            nc.gpsimd.memset(ones[:, :], 1.0)
            pool.wait_ge(S["const_loaded"], 32)
            nc.gpsimd.tensor_copy(before[:, :], const("before"))
            nc.gpsimd.tensor_copy(seen[0][:, 0, :], const("start")).then_inc(S["rank_consts"], 1)
            for a in range(2):
                nc.gpsimd.tensor_copy(row[a][:, :, TOKEN], const("ids")[:, TT * a:TT * a + TT]).then_inc(S["id_start"], 1)
            pool.wait_ge(S["id_start"], 2)
            pool.wait_ge(S["rank_consts"], 1)

            def step(s, a, turn, now=True, prev=True, nxt=True, old=True):
                n = 1 - a
                if old:
                    pool.wait_ge(S["onehot_ready"], s - 1)
                    if not (isinstance(s, int) and s < 3):
                        pool.wait_ge(S["rank_done"], s - 2)
                    for t in range(TT):
                        after = seen[a][:, t + 1, :] if t + 1 < TT else seen[n][:, 0, :]
                        nc.gpsimd.tensor_tensor(after, seen[a][:, t, :], onehot[a][:, t * E:(t + 1) * E], ALU.add).then_inc(S["seen_ready"], 1)
                        pool.wait_ge(S["seen_ready"], TT * (s - 2) + t + 1)
                if prev:
                    if not (isinstance(s, int) and s < 3):
                        pool.wait_ge(scattered[n], 16 * TT * (turn - 2))
                    pool.nop(nofuse=True)
                    nc.gpsimd.tensor_scalar_add(row[n][:, :, TOKEN], row[n][:, :, TOKEN], float(2 * TT * P)).then_inc(S["id_ready"], 1)
                if old:
                    pool.wait_ge(S["pos_ready"], s - 1)
                    pool.wait_ge(S["id_ready"], s - 1)
                    pool.nop(nofuse=True)
                    for t in range(TT):
                        pool.indirect_dma_start(sorted_rows, bass.IndirectOffsetOnAxis(ap=pos[a][:, t:t + 1], axis=0),
                                                row[a][:, t, :], None, bounds_check=E * REGION - 1, oob_is_err=False
                                                ).then_inc(scattered[a], 16)
                if nxt:
                    pool.wait_ge(S["h_ready"], s + 2)
                    if prev:
                        pool.wait_ge(S["h2_ready"], 2 * s)
                    for t in range(TT):
                        ins = nc.gpsimd.tensor_tensor(hb[n][:, t * C:(t + 1) * C], h[n][:, t * C:(t + 1) * C],
                                                      bias_bc[:, :], ALU.add)
                    ins.then_inc(S["hb_ready"], 1)

            run_steps(pool, step)

            def tile(j, u, turn):
                if there(j):
                    pool.wait_ge(S["y_ready"], j + 1)
                    pool.nop(nofuse=True)
                    pool.indirect_dma_start(out_rows, bass.IndirectOffsetOnAxis(ap=token[u][:, 0:1], axis=0),
                                            y[u], None, bounds_check=NTOK - 1, oob_is_err=False
                                            ).then_inc(y_stored[u], 16)

            run_tiles(pool, tile)

        @block.scalar
        def _(act):
            act.wait_ge(S["filt_ps"], 1)
            nc.scalar.activation(filt[:, :, :], b4[:, 0:3 * GRP].rearrange("p (m o) -> p m o", o=GRP), ACT.Copy).then_inc(S["filt_ready"], 1)

            def norm(dst, src, rstd, shift, ready):
                for t in range(TT):
                    nc.scalar.activation(dst[:, t, :], src(t), ACT.Identity, bias=shift(t), scale=rstd(t)).then_inc(S[ready], 1)

            def heads(ap):
                return ap.rearrange("p (g c) -> p g c", c=GRP)

            def step(s, a, turn, now=True, prev=True, nxt=True, old=True):
                n = 1 - a
                if nxt:
                    act.wait_ge(S["conv_done"], s + 2)
                    if prev:
                        act.wait_ge(S["hb_ready"], s)
                    nc.scalar.activation(h[n][:, :], conv_flat[:, 0:TT * C], ACT.Copy).then_inc(S["h_ready"], 1)
                if old:
                    act.wait_ge(S["t2_done"], s - 1)
                    nc.scalar.activation(x2T[a][:, :, :], tr_ps[:, :, 0:TT * P], ACT.Copy).then_inc(S["x2T_ready"], 1)
                if prev:
                    for m, bank in enumerate((b4, b5)):
                        act.wait_ge(S["at_done"], KC * (s - 1) + m + 1)
                        nc.scalar.activation(attT_hi[n][:, m, :], bank[:, 0:TT * P], ACT.Copy).then_inc(S["attT_hi_ready"], 1)
                if nxt:
                    act.wait_ge(S["var1_ready"], s + 2)
                    nc.scalar.activation(std1[n][:, :], mv1[n][:, :, 1], ACT.Sqrt, bias=eps_t[:, 0:1]).then_inc(S["std1_ready"], 1)
                    act.wait_ge(S["shift1_ready"], s + 2)
                    norm(xn1[n], lambda t: h[n][:, t * C:(t + 1) * C], lambda t: rstd1[n][:, t:t + 1],
                         lambda t: shift1[n][:, t:t + 1], "xn1_ready")
                if now:
                    act.wait_ge(S["kv_ones"], 4)
                    act.wait_ge(S["kv_done"], TT * s + 1)
                    nc.scalar.activation(kv[a][:, 0, :, 0:GRP], heads(b7[:, :]), ACT.Relu).then_inc(S["kv_ready"], 1)
                    act.wait_ge(S["kv_done"], TT * s + 2)
                    nc.scalar.activation(kv[a][0:64, 1, :, 0:GRP], heads(b4[0:64, :]), ACT.Relu)
                    nc.scalar.activation(kv[a][64:P, 2, :, 0:GRP], heads(b4[64:P, :]), ACT.Relu).then_inc(S["kv_ready"], 1)
                    act.wait_ge(S["kv_done"], TT * s + 3)
                    nc.scalar.activation(kv[a][:, 3, :, 0:GRP], heads(b5[:, :]), ACT.Relu).then_inc(S["kv_ready"], 1)
                    act.wait_ge(S["q_done"], KC * s + 1)
                    nc.scalar.activation(qT[a][:, 0, :], b6[:, 0:TT * P], ACT.Relu).then_inc(S["q0_ready"], 1)
                    act.wait_ge(S["q_done"], KC * s + 2)
                    nc.scalar.activation(qT[a][:, 1, :], b7[:, 0:TT * P], ACT.Relu).then_inc(S["q1_ready"], 1)
                if nxt:
                    act.wait_ge(S["t1_done"], s + 2)
                    nc.scalar.activation(xT_hi[n][:, :, :], tr_ps[:, :, 0:TT * P], ACT.Copy).then_inc(S["xT_hi_ready"], 1)
                if prev:
                    act.wait_ge(S["var2_ready"], s)
                    nc.scalar.activation(std2[n][:, :], mv2[n][:, :, 1], ACT.Sqrt, bias=eps_t[:, 0:1]).then_inc(S["std2_ready"], 1)
                    act.wait_ge(S["shift2_ready"], s)
                    norm(xn2[n], lambda t: row[n][:, t, 0:C], lambda t: row[n][:, t, RSTD:RSTD + 1],
                         lambda t: row[n][:, t, SHIFT:SHIFT + 1], "xn2_ready")

            run_steps(act, step)

            def tile(j, u, turn):
                if there(j + 2):
                    v = (u + 2) % 4
                    act.wait_ge(S["st_done"], j + 3)
                    nc.scalar.activation(sT_hi[v], (b4, b5)[v % 2][:, 0:C].rearrange("p (k t) -> p k t", k=KC), ACT.Copy).then_inc(S["sT_hi_ready"], 1)
                if there(j + 4):
                    r, v = (u + 4) % RING, u % 4
                    act.wait_ge(srow_loaded[r], 16 * (turn + 1 + (u + 4) // RING))
                    nc.scalar.activation(sxn[v], srow[r][:, 0:C], ACT.Identity, bias=srow[r][:, SHIFT:SHIFT + 1],
                                         scale=srow[r][:, RSTD:RSTD + 1]).then_inc(S["sxn_ready"], 1)

            run_tiles(act, tile)

        @block.vector
        def _(dve):
            nc.vector.memset(eps_t[:, :], EPS)
            nc.vector.memset(past[:, :, 0:1], 1.0)
            dve.wait_ge(S["taps_loaded"], 32)
            for k in range(TAPS):
                nc.vector.tensor_scalar(tap_terms[:, k, :], taps[:, :], float(k), h0_bc[:, k:k + 1], ALU.is_equal, ALU.mult).then_inc(S["filt_terms"], 1)
            dve.wait_ge(S["filt_terms"], TAPS)
            dve.wait_ge(S["levels_zero"], 1)
            terms = tap_terms.rearrange("p k x -> p x k")
            nc.vector.tensor_reduce(levels[:, 0:SPAN], terms[:, 0:SPAN, :], AX_X, ALU.add)
            nc.vector.tensor_reduce(second[:, :], terms[:, SPAN:, :], AX_X, ALU.add).then_inc(S["filt_levels"], 1)

            def split_weights():
                dve.wait_ge(S["w_loaded"], 4 * 16)
                for k in range(KC):
                    nc.vector.tensor_copy(wqkv_hi[:, k, :], wqkv[k]).then_inc(S["w_hi"], 1)
                nc.vector.tensor_copy(wproj_hi[:, :, :], wproj).then_inc(S["w_hi"], 1)
                dve.wait_ge(S["w_hi"], KC + 1)
                for k in range(KC):
                    nc.vector.tensor_tensor(wqkv_lo[:, k, :], wqkv[k], wqkv_hi[:, k, :].bitcast(F32), ALU.subtract)
                nc.vector.tensor_tensor(wproj_lo[:, :, :], wproj, wproj_hi[:, :, :].bitcast(F32), ALU.subtract).then_inc(S["w_split"], 1)
                dve.wait_ge(S["const_loaded"], 32)

            def split_experts(k):
                dve.wait_ge(S["wexp_loaded"], 16 * (k + 1))
                own_channel = wexp.rearrange("p (e c) -> p e c", c=C)[:, :, k * P:(k + 1) * P]
                nc.vector.tensor_tensor(own_channel, own_channel, ident.rearrange("p (a c) -> p a c", a=1).to_broadcast([P, E, P]), ALU.add).then_inc(S["wexp_plus"], 1)
                dve.wait_ge(S["wexp_plus"], k + 1)
                nc.vector.tensor_copy(wexp_hi[:, k, :], wexp).then_inc(S["wexp_hi_ready"], 1)
                dve.wait_ge(S["wexp_hi_ready"], k + 1)
                nc.vector.tensor_tensor(wexp_lo[:, k, :], wexp, wexp_hi[:, k, :].bitcast(F32), ALU.subtract).then_inc(S["wexp_split"], 1)

            def stats(src, st, cnt, done):
                for t in range(TT):
                    nc.vector.bn_stats(st[:, t, :], src(t)).then_inc(S[done], 1)

            def mean_var(st, mv, cnt, done, ready):
                dve.wait_ge(S[done], TT * cnt)
                dve.nop(nofuse=True)
                for t in range(TT):
                    ins = nc.vector.bn_aggr(mv[:, t, :], st[:, t, :])
                ins.then_inc(S[ready], 1)

            def rstd_shift(mv, std, rstd, shift, cnt, std_ready, rstd_ready, shift_ready):
                dve.wait_ge(S[std_ready], cnt)
                nc.vector.reciprocal(rstd, std[:, :]).then_inc(S[rstd_ready], 1)
                dve.wait_ge(S[rstd_ready], cnt)
                nc.vector.scalar_tensor_tensor(shift, mv[:, :, 0], -1.0, rstd, ALU.mult, ALU.mult).then_inc(S[shift_ready], 1)

            def step(s, a, turn, now=True, prev=True, nxt=True, old=True):
                n = 1 - a
                if nxt:
                    dve.wait_ge(S["h_ready"], s + 2)
                    stats(lambda t: h[n][:, t * C:(t + 1) * C], stats1[n], s + 2, "stats1_done")
                    mean_var(stats1[n], mv1[n], s + 2, "stats1_done", "var1_ready")
                if prev:
                    for m, bank in enumerate((b4, b5)):
                        dve.wait_ge(S["attT_hi_ready"], KC * (s - 1) + m + 1)
                        nc.vector.tensor_tensor(attT_lo[n][:, m, :], bank[:, 0:TT * P], attT_hi[n][:, m, :].bitcast(F32), ALU.subtract).then_inc(S["attT_lo_ready"], 1)
                if nxt:
                    rstd_shift(mv1[n], std1[n], rstd1[n][:, :], shift1[n][:, :], s + 2, "std1_ready", "rstd1_ready", "shift1_ready")
                if old:
                    sc3 = score[a][:, :].rearrange("p (t e) -> p t e", e=E)
                    k3 = key[a][:, :].rearrange("p (t e) -> p t e", e=E)
                    o3 = onehot[a][:, :].rearrange("p (t e) -> p t e", e=E)

                    def spread(v):
                        return v[:, :].rearrange("p (t o) -> p t o", o=1).to_broadcast([P, TT, E])
                    dve.wait_ge(S["score_done"], s - 1)
                    nc.vector.tensor_copy(score[a][:, :], b6[:, 0:TT * E]).then_inc(S["score_copied"], 1)
                    dve.wait_ge(S["score_copied"], s - 1)
                    nc.vector.tensor_reduce(smax[a][:, :], sc3, AX_X, ALU.max).then_inc(S["smax_ready"], 1)
                    dve.wait_ge(S["smax_ready"], s - 1)
                    nc.vector.tensor_tensor(k3, sc3, spread(smax[a]), ALU.is_equal).then_inc(S["eq_ready"], 1)
                    dve.wait_ge(S["eq_ready"], s - 1)
                    nc.vector.tensor_tensor(key[a][:, :], key[a][:, :], const("tie"), ALU.mult).then_inc(S["key_ready"], 1)
                    dve.wait_ge(S["key_ready"], s - 1)
                    nc.vector.tensor_reduce(kmax[a][:, :], k3, AX_X, ALU.max).then_inc(S["kmax_ready"], 1)
                    dve.wait_ge(S["kmax_ready"], s - 1)
                    nc.vector.tensor_tensor(o3, k3, spread(kmax[a]), ALU.is_equal).then_inc(S["onehot_ready"], 1)
                    dve.wait_ge(S["rank_done"], s - 1)
                    nc.vector.tensor_tensor(place[a][:, :], conv_ps[:, 1, RANK:RANK + TT * E], onehot[a][:, :], ALU.mult).then_inc(S["place_ready"], 1)
                    dve.wait_ge(S["place_ready"], s - 1)
                    nc.vector.tensor_reduce(pos_sum[a][:, :], place[a][:, :].rearrange("p (t e) -> p t e", e=E), AX_X, ALU.add).then_inc(S["pos_summed"], 1)
                    dve.wait_ge(S["pos_summed"], s - 1)
                    nc.vector.tensor_copy(pos[a][:, :], pos_sum[a][:, :]).then_inc(S["pos_ready"], 1)
                if prev:
                    dve.wait_ge(S["hb_ready"], s)
                    if not (isinstance(s, int) and s < 3):
                        dve.wait_ge(scattered[n], 16 * TT * (turn - 2))
                    dve.wait_ge(S["proj_done"], 2 * s - 1)
                    nc.vector.tensor_tensor(row[n][:, 0:2, 0:C], b4[:, :].rearrange("p (t c) -> p t c", c=C),
                                            hb[n][:, 0:2 * C].rearrange("p (t c) -> p t c", c=C), ALU.add).then_inc(S["h2_ready"], 1)
                    dve.wait_ge(S["proj_done"], 2 * s)
                    nc.vector.tensor_tensor(row[n][:, 2, 0:C], b5[:, 0:C], hb[n][:, 2 * C:3 * C], ALU.add).then_inc(S["h2_ready"], 1)
                    dve.wait_ge(S["h2_ready"], 2 * s)
                    stats(lambda t: row[n][:, t, 0:C], stats2[n], s, "stats2_done")
                if now:
                    dve.wait_ge(S["vk_done"], s + 1)
                    vk = b6[:, 0:4 * (GRP + 1)].rearrange("p (i e) -> p i e", e=GRP + 1)
                    bd_all = bd[a][:, :, :, :].rearrange("p b m e -> p (b m) e")
                    for i in range(4):
                        nc.vector.tensor_tensor(bd_all[:, i, 0:P].rearrange("p (g e) -> p g e", e=GRP),
                                                vk[:, i:i + 1, 0:GRP].to_broadcast([P, P // GRP, GRP]),
                                                mask[:, 0:P].rearrange("p (g e) -> p g e", e=GRP), ALU.mult)
                    nc.vector.tensor_tensor(bd_all[:, :, P:], mask[:, P:].rearrange("p (a e) -> p a e", a=1).to_broadcast([P, 4, HPG]),
                                            vk[:, :, GRP:].to_broadcast([P, 4, HPG]), ALU.mult).then_inc(S["bd_ready"], 1)
                if prev:
                    mean_var(stats2[n], mv2[n], s, "stats2_done", "var2_ready")
                if nxt:
                    dve.wait_ge(S["xT_hi_ready"], s + 2)
                    nc.vector.tensor_tensor(xT_lo[n][:, :, :], tr_ps[:, :, 0:TT * P], xT_hi[n][:, :, :].bitcast(F32), ALU.subtract).then_inc(S["xT_lo_ready"], 1)
                if prev:
                    rstd_shift(mv2[n], std2[n], row[n][:, :, RSTD], row[n][:, :, SHIFT], s, "std2_ready", "rstd2_ready", "shift2_ready")
                if now:
                    nds = [bank[:, 0:KC * (P + HPG)].rearrange("p (m e) -> p m e", e=P + HPG) for bank in (b7, b4, b5)]
                    for t, nd in enumerate(nds):
                        dve.wait_ge(S["vkq_done"], TT * s + t + 1)
                        nc.vector.tensor_scalar_add(den[a][:, t, :].rearrange("p (m e) -> p m e", e=HPG), nd[:, :, P:], DEN_EPS).then_inc(S["den_copied"], 1)
                    for t in range(TT):
                        dve.wait_ge(S["den_copied"], TT * s + t + 1)
                        nc.vector.reciprocal(rden[a][:, t, :], den[a][:, t, :]).then_inc(S["rden_ready"], 1)
                    for t, nd in enumerate(nds):
                        dve.wait_ge(S["rden_ready"], TT * s + t + 1)
                        for m in range(KC):
                            ins = nc.vector.tensor_tensor(
                                att[a][:, t, m * P:(m + 1) * P].rearrange("p (g e) -> p g e", e=HD),
                                nd[:, m, 0:P].rearrange("p (g e) -> p g e", e=HD),
                                rden[a][:, t, m * HPG:(m + 1) * HPG].rearrange("p (g o) -> p g o", o=1).to_broadcast([P, HPG, HD]),
                                ALU.mult)
                        ins.then_inc(S["att_ready"], 1)
                if isinstance(s, int) and s == -1:
                    split_weights()
                if isinstance(s, int) and s in (0, 1):
                    split_experts(s)

            run_steps(dve, step)

            steps = [0]

            def link(ins):
                steps[0] += 1
                ins.then_inc(S["plan_step"], 1)
                dve.wait_ge(S["plan_step"], steps[0])

            def over(v, n, m):
                return v.rearrange("p (a m) -> p a m", a=1).to_broadcast([P, n, m])

            def each(v, n, m):
                return v.rearrange("p (n a) -> p n a", a=1).to_broadcast([P, n, m])

            F = NTOK // P
            total = conv_ps[:, 1, RANK:RANK + E]
            dve.wait_ge(S["total_done"], 1)
            nc.vector.tensor_scalar_add(last_row[:, :], total, -float(P))
            link(nc.vector.tensor_tensor(count[:, :], total, const("base"), ALU.subtract))
            link(nc.vector.tensor_tensor(more[:, :, :], each(count[:, :], E, F), over(const("full"), E, F), ALU.is_gt))
            link(nc.vector.tensor_reduce(full_tiles[:, :], more[:, :, :], AX_X, ALU.add))
            link(nc.vector.tensor_tensor(upto[:, :, :], over(full_tiles[:, :], E, E), const("upto").rearrange("p (e f) -> p e f", f=E), ALU.mult))
            link(nc.vector.tensor_reduce(ends[:, :], upto[:, :, :], AX_X, ALU.add))
            link(nc.vector.tensor_tensor(starts[:, :], ends[:, :], full_tiles[:, :], ALU.subtract))
            nc.vector.scalar_tensor_tensor(first_row[:, :], starts[:, :], -float(P), const("base"), ALU.mult, ALU.add)
            link(nc.vector.tensor_tensor(past[:, :, 1:], over(ends[:, :], TILES, E), each(const("tile"), TILES, E), ALU.is_le))
            nc.vector.tensor_reduce(expert[:, :], past[:, :, 1:], AX_X, ALU.add)
            link(nc.vector.tensor_tensor(own[:, :, :], past[:, :, 0:E], past[:, :, 1:], ALU.subtract))
            nc.vector.tensor_scalar(w_off[:, :], expert[:, :], float(E - 1), float(C), ALU.min, ALU.mult)
            nc.vector.tensor_tensor(own_first[:, :, :], own[:, :, :], over(first_row[:, :], TILES, E), ALU.mult)
            link(nc.vector.tensor_tensor(own_last[:, :, :], own[:, :, :], over(last_row[:, :], TILES, E), ALU.mult))
            nc.vector.tensor_reduce(row_at[:, :], own_first[:, :, :], AX_X, ALU.add)
            link(nc.vector.tensor_reduce(row_end[:, :], own_last[:, :, :], AX_X, ALU.add))
            link(nc.vector.tensor_tensor(row_at[:, :], row_at[:, :], const("rows"), ALU.add))
            link(nc.vector.tensor_tensor(row_from[:, :], row_at[:, :], row_end[:, :], ALU.min))
            nc.vector.tensor_copy(r_off[:, :], row_from[:, :])
            link(nc.vector.tensor_tensor(twice[:, :], row_at[:, :], row_from[:, :], ALU.subtract))
            nc.vector.tensor_scalar(skip[:, :], twice[:, :], const("lane"), float(BIG), ALU.is_gt, ALU.mult).then_inc(S["plan_ready"], 1)
            dve.wait_ge(S["plan_ready"], 1)

            def tile(j, u, turn):
                if there(j + 2):
                    v = (u + 2) % 4
                    dve.wait_ge(S["sT_hi_ready"], j + 3)
                    nc.vector.tensor_tensor(sT_lo[v], (b4, b5)[v % 2][:, 0:C].rearrange("p (k t) -> p k t", k=KC),
                                            sT_hi[v].bitcast(F32), ALU.subtract).then_inc(S["sT_lo_ready"], 1)
                if there(j):
                    if not (isinstance(j, int) and j < RING):
                        dve.wait_ge(y_stored[u], 16 * turn)
                    nc.vector.tensor_tensor(token[u][:, :], srow[u][:, TOKEN:TOKEN + 1], skip[:, bass.ds(j, 1)], ALU.add)
                    dve.wait_ge(S["expert_done"], j + 1)
                    nc.vector.tensor_tensor(y[u], (b6, b7)[u % 2][:, 0:C], srow[u][:, 0:C], ALU.add).then_inc(S["y_ready"], 1)

            run_tiles(dve, tile)

        @block.tensor
        def _(pe):
            pe.wait_ge(S["filt_levels"], 1)
            nc.tensor.matmul(b4[:, 0:GRP], levels[:, LEAD:LEAD + P], second[:, :], start=True, stop=True)
            nc.tensor.matmul(b4[:, GRP:2 * GRP], levels[:, 0:P], second[:, :], start=True, stop=True)
            nc.tensor.matmul(b4[:, 2 * GRP:3 * GRP], levels[:, P:2 * P], second[:, :], start=True, stop=True).then_inc(S["filt_ps"], 1)
            pe.wait_ge(S["filt_ready"], 1)

            def conv(a, x_count):
                pe.wait_ge(x_loaded[a], x_count)

                def rows(q, further):
                    t, g = divmod(q, 4)
                    inner = 0 < q % NJ < NJ - 1
                    return nc.tensor.matmul(conv_flat[GRP * g:GRP * (g + 1), t * C:(t + 1) * C],
                                            filt[:, 2 if further else 0 if q % NJ == 0 else 1, :],
                                            xb[a][:, q + 1 if further else q, :], start=not further,
                                            stop=further or not inner, tile_position=(0, GRP * g))

                for q, further in [(0, 0), (1, 0), (2, 0), (3, 0), (4, 0), (1, 1), (2, 1), (3, 1), (4, 1), (5, 0),
                                   (6, 0), (7, 0), (8, 0), (9, 0), (10, 0), (11, 0), (8, 1), (9, 1), (10, 1), (7, 1)]:
                    ins = rows(q, bool(further))
                ins.then_inc(S["conv_done"], 1)

            def flip(dst, src, s_ready, base):
                for t in range(TT):
                    pe.wait_ge(S[s_ready], base + t + 1)
                    for m in range(KC):
                        ins = nc.tensor.transpose(dst(m)[:, t * P:(t + 1) * P], src[:, t, m * P:(m + 1) * P], ident)
                return ins

            def split_product(o, lhsT, rhs):
                terms = [(l, r, k) for k in range(KC) for l, r in ((0, 0), (0, 1), (1, 0))]
                for i, (l, r, k) in enumerate(terms):
                    ins = nc.tensor.matmul(o, lhsT[l](k), rhs[r](k), start=i == 0, stop=i == len(terms) - 1)
                return ins

            def step(s, a, turn, now=True, prev=True, nxt=True, old=True):
                n = 1 - a
                if nxt:
                    if now:
                        pe.wait_ge(S["h_ready"], s + 1)
                    if not (isinstance(s, int) and s < 3):
                        pe.wait_ge(S["place_ready"], s - 2)
                    conv(n, 48 * turn)
                if isinstance(s, int) and s == -1:
                    pe.wait_ge(S["const_loaded"], 32)
                if old:
                    if now:
                        pe.wait_ge(S["xT_lo_ready"], s + 1)
                    flip(lambda m: tr_ps[:, m, :], xn2[a], "xn2_ready", TT * (s - 2)).then_inc(S["t2_done"], 1)
                if prev:
                    pe.wait_ge(S["att_ready"], TT * s)
                    for m, bank in enumerate((b4, b5)):
                        for t in range(TT):
                            ins = nc.tensor.transpose(bank[:, t * P:(t + 1) * P], att[n][:, t, m * P:(m + 1) * P], ident)
                        ins.then_inc(S["at_done"], 1)
                if old:
                    pe.wait_ge(S["x2T_ready"], s - 1)
                    for t in range(TT):
                        for k in range(KC):
                            ins = nc.tensor.matmul(b6[:, t * E:(t + 1) * E], x2T[a][:, k, t * P:(t + 1) * P], gate[:, k, :],
                                                   start=k == 0, stop=k == KC - 1)
                    ins.then_inc(S["score_done"], 1)
                if now:
                    if isinstance(s, int) and s == 0:
                        pe.wait_ge(S["w_split"], 1)
                    pe.wait_ge(S["xT_lo_ready"], s + 1)
                    for t, bank in enumerate((b7, b4, b5)):
                        if prev and t > 0:
                            pe.wait_ge(S["attT_lo_ready"], KC * (s - 1) + t)
                        split_product(bank[:, :], [lambda k, x=x: x[:, k, t * P:(t + 1) * P] for x in (xT_hi[a], xT_lo[a])],
                                      [lambda k, w=w: w[:, k, C:] for w in (wqkv_hi, wqkv_lo)]).then_inc(S["kv_done"], 1)
                    for m, bank in enumerate((b6, b7)):
                        if m == 0 and old:
                            pe.wait_ge(S["score_copied"], s - 1)
                        if m == 1:
                            pe.wait_ge(S["kv_ready"], TT * s + 1)
                        split_product(bank[:, 0:TT * P], [lambda k, w=w: w[:, k, m * P:(m + 1) * P] for w in (wqkv_hi, wqkv_lo)],
                                      [lambda k, x=x: x[:, k, :] for x in (xT_hi[a], xT_lo[a])]).then_inc(S["q_done"], 1)
                if old:
                    if nxt:
                        pe.wait_ge(S["h_ready"], s + 2)
                    pe.wait_ge(S["seen_ready"], TT * (s - 1))
                    o = conv_ps[:, 1, RANK:RANK + TT * E]
                    nc.tensor.matmul(o, before[:, :], onehot[a][:, :], start=True, stop=False)
                    nc.tensor.matmul(o, ones[:, :], seen[a][:, :, :].rearrange("p t e -> p (t e)"), start=False, stop=True).then_inc(S["rank_done"], 1)
                if prev:
                    pe.wait_ge(S["attT_lo_ready"], KC * s)
                    for t in range(TT):
                        if now and t != 1:
                            pe.wait_ge(S["kv_ready"], TT * s + 2 + t // 2)
                        o = b4[:, t * C:(t + 1) * C] if t < 2 else b5[:, 0:C]
                        ins = split_product(o, [lambda k, x=x: x[:, k, t * P:(t + 1) * P] for x in (attT_hi[n], attT_lo[n])],
                                            [lambda k, w=w: w[:, k, :] for w in (wproj_hi, wproj_lo)])
                        if t > 0:
                            ins.then_inc(S["proj_done"], 1)
                if now:
                    pe.wait_ge(S["kv_ready"], TT * s + TT)
                    pe.wait_ge(S["q0_ready"], s + 1)
                    for b in range(2):
                        for m in range(KC):
                            i = KC * b + m
                            for k, seg in enumerate(((0, 1), (3, 2))[b]):
                                for g in range(4):
                                    ins = nc.tensor.matmul(b6[GRP * g:GRP * (g + 1), i * (GRP + 1):(i + 1) * (GRP + 1)],
                                                           kv[a][:, seg, 4 * m + g, 0:GRP], kv[a][:, seg, NG + 4 * m + g, :],
                                                           start=k == 0, stop=k == 1, tile_position=(0, GRP * g))
                    ins.then_inc(S["vk_done"], 1)
                if nxt:
                    flip(lambda m: tr_ps[:, m, :], xn1[n], "xn1_ready", TT * (s + 1)).then_inc(S["t1_done"], 1)
                if now:
                    pe.wait_ge(S["bd_ready"], s + 1)
                    pe.wait_ge(S["q1_ready"], s + 1)
                    if prev:
                        pe.wait_ge(S["h2_ready"], 2 * s)
                    for t, bank in enumerate((b7, b4, b5)):
                        for m in range(KC):
                            o = bank[:, m * (P + HPG):(m + 1) * (P + HPG)]
                            if t == 1:
                                for b in range(2):
                                    ins = nc.tensor.matmul(o[64 * b:64 * b + 64, :], qT[a][:, m, P + 64 * b:P + 64 * b + 64],
                                                           bd[a][:, b, m, :], start=True, stop=True, tile_position=(0, 64 * b))
                            else:
                                ins = nc.tensor.matmul(o, qT[a][:, m, t * P:(t + 1) * P], bd[a][:, t // 2, m, :],
                                                       start=True, stop=True)
                        ins.then_inc(S["vkq_done"], 1)

            pe.wait_ge(S["rank_consts"], 1)
            run_steps(pe, step)

            pe.wait_ge(S["seen_ready"], TT * NP)
            pe.wait_ge(S["place_ready"], NP)
            nc.tensor.matmul(conv_ps[:, 1, RANK:RANK + E], ones[:, :], seen[0][:, 0, :], start=True, stop=True).then_inc(S["total_done"], 1)
            pe.wait_ge(S["plan_ready"], 1)
            pe.wait_ge(S["wexp_split"], KC)

            def tile(j, u, turn):
                if there(j + 3):
                    v = (u + 3) % 4
                    if not (isinstance(j, int) and j < -1):
                        pe.wait_ge(S["sT_lo_ready"], j + 2)
                    pe.wait_ge(S["sxn_ready"], j + 4)
                    for m in range(KC):
                        ins = nc.tensor.transpose((b4, b5)[v % 2][:, m * P:(m + 1) * P], sxn[v][:, m * P:(m + 1) * P], ident)
                    ins.then_inc(S["st_done"], 1)
                if there(j + 1):
                    v = (u + 1) % 4
                    off = pe.value_load(w_off[0:1, bass.ds(j + 1, 1)], min_val=0, max_val=(E - 1) * C)
                    if not (isinstance(j, int) and j < 1):
                        pe.wait_ge(S["y_ready"], j)
                    pe.wait_ge(S["sT_lo_ready"], j + 2)
                    split_product((b6, b7)[v % 2][:, 0:C], [lambda k, x=x: x[:, k, :] for x in (sT_hi[v], sT_lo[v])],
                                  [lambda k, x=x: x[:, k, bass.ds(off, C)] for x in (wexp_hi, wexp_lo)]).then_inc(S["expert_done"], 1)

            run_tiles(pe, tile)


_INS = ['x', 'L0_tok_h0', 'L0_attn_qkv_weight', 'L0_attn_proj_weight', 'L0_attn_proj_bias', 'L0_ffn_gate_w', 'L0_ffn_expert_w']
_OUTS = [((16, 192, 256), 'float32')]


def kernel(**inputs):
    import numpy as _np
    import concourse.bacc as _bacc
    from concourse import mybir as _mybir
    from concourse.bass_utils import run_bass_kernel_spmd as _run

    put = {
        "x": inputs["x"],
        "h0": inputs["L0_tok_h0"],
        "wqkvT": _np.transpose(inputs["L0_attn_qkv_weight"]),
        "wprojT": _np.transpose(inputs["L0_attn_proj_weight"]),
        "bias": inputs["L0_attn_proj_bias"],
        "gateT": _np.transpose(inputs["L0_ffn_gate_w"]),
        "wexpT": _np.transpose(inputs["L0_ffn_expert_w"], (2, 0, 1)).reshape(C, E * C),
    }
    mid = _np.arange(2 * (GRP - 1) + TAPS)[:, None]
    tap = _np.concatenate([_np.arange(4 * (GRP - 1) + 3 * (TAPS - 1) + 1)[None, :] - 2 * mid, mid - 2 * _np.arange(GRP)[None, :]], axis=1)
    put_tap = _np.where((tap >= 0) & (tap < TAPS), tap, -1).astype(_np.float32)
    lane = _np.arange(P)[:, None]
    e = _np.arange(E)
    columns = {
        "ident": lane == _np.arange(P),
        "mask": _np.concatenate([lane // HD == _np.arange(P) // HD, lane // HD == _np.arange(P // HD)], axis=1),
        "tie": _np.tile(_np.arange(E, 0, -1), 3),
        "ids": lane + P * _np.arange(6) - 6 * P,
        "start": e * (REGION // P) + 1,
        "before": lane < _np.arange(P),
        "full": P * _np.arange(3072 // P),
        "upto": (_np.arange(E)[None, :] <= e[:, None]).reshape(-1),
        "tile": _np.arange(TILES),
        "rows": P * _np.arange(TILES),
        "base": e * REGION + P,
        "lane": lane,
    }
    packed = _np.zeros((P, NCONST), _np.float32)
    for name, (lo, hi) in CONSTS.items():
        packed[:, lo:hi] = columns[name]
    put["const_c"] = packed
    put["tap_c"] = put_tap

    nc = _bacc.Bacc("TRN2", target_bir_lowering=False, num_devices=1)
    arrays, args = {}, []
    for name, a in put.items():
        a = _np.ascontiguousarray(a)
        arrays[f"in_{name}_dram"] = a
        args.append(nc.dram_tensor(f"in_{name}_dram", a.shape, _mybir.dt.from_np(a.dtype), kind="ExternalInput").ap())
    for i, (shape, dtype) in enumerate(_OUTS):
        dt = _mybir.dt.from_np(_np.dtype(dtype))
        args.append(nc.dram_tensor(f"out_{i}_dram", shape, dt, kind="ExternalOutput").ap())
    audio_tower(nc, *args)
    r = _run(nc, [arrays], core_ids=[0])
    return r.results[0]["out_0_dram"]
```

```python
from contextlib import ExitStack

import concourse.bass as bass
from concourse import mybir

F32 = mybir.dt.float32
F32R = mybir.dt.float32r
BF16 = mybir.dt.bfloat16
I32 = mybir.dt.int32
U32 = mybir.dt.uint32
ALU = mybir.AluOpType
ACT = mybir.ActivationFunctionType
AX_X = mybir.AxisListType.X

P = 128
C = 256
KC = C // P
TAPS = 8
GRP = 32
HD = 8
E = 8
EPS = 1e-5
DEN_EPS = 1e-15

TILES = 3072 // P + E - 1
EARLY = -((E * (P - 1) - (3072 - 2 * 384)) // P)
ROUND = 1.5 * 2 ** 23
HALF = 0.5 - 0.5 / P
REGION = 3072 + P
BIG = 1 << 20
RSTD, SHIFT, TOKEN = C, C + 1, C + 2
ROW = C + 3
RING = 8
WLEAD = RING - 1

CONSTS = {}
_at = 0
for _name, _width in (("ident", P), ("mask", P + P // HD), ("tie", 3 * E), ("ids", 2 * 3), ("start", E), ("before", P),
                      ("upto", E * E), ("tile", TILES), ("rows", TILES), ("base", E), ("lane", 1)):
    CONSTS[_name] = (_at, _at + _width)
    _at += _width
NCONST = _at


def audio_tower(nc, x, taps, wqkvT, wprojT, bias, gateT, wexpT, const_c, out):
    B, N, _ = x.shape
    NL1 = (N + TAPS - 1) // 2
    NT = (NL1 + TAPS - 1) // 2
    NJ = NT // GRP
    NP = B // 2
    TT = 2 * NT // P
    Q = 2 * NJ
    LEAD = 3 * (TAPS - 2)
    SPAN = 4 * (GRP - 1) + 3 * (TAPS - 1) + 1
    EXTRA = SPAN - P
    FIRST = P - EXTRA
    MID = 2 * (GRP - 1) + TAPS
    RANK = 448
    NG = C // GRP
    HPG = P // HD
    assert NT % GRP == 0 and (2 * NT) % P == 0 and TT == 3 and FIRST == 4 * GRP - LEAD
    assert FIRST + P * (NJ - 1) == N and NT == 3 * 64

    xp = x.rearrange("(s b) n c -> s n b c", b=2)
    out_rows = out.rearrange("b t c -> (b t) c")
    NTOK = B * NT
    assert NTOK == 3072
    sorted_rows = nc.dram_tensor("sorted_rows", (E * REGION, ROW), F32, kind="Internal").ap()

    with ExitStack() as ctx:
        def sb(name, shape, dt=F32):
            return ctx.enter_context(nc.sbuf_tensor(name, shape, dt))

        def sem(name):
            return ctx.enter_context(nc.semaphore(name))

        def two(name, shape, dt=F32):
            return [sb(f"{name}{i}", shape, dt) for i in range(2)]

        gate = sb("gate", [P, KC, E])
        wqkv_hi, wqkv_lo = sb("wqkv_hi", [P, KC, 3 * C], F32R), sb("wqkv_lo", [P, KC, 3 * C], F32R)
        wproj_hi, wproj_lo = sb("wproj_hi", [P, KC, C], F32R), sb("wproj_lo", [P, KC, C], F32R)
        wexp_hi, wexp_lo = sb("wexp_hi", [P, KC, E * C], F32R), sb("wexp_lo", [P, KC, E * C], F32R)
        bias_bc = sb("bias_bc", [P, C])
        consts = sb("consts", [P, NCONST])

        def const(name):
            return consts[:, CONSTS[name][0]:CONSTS[name][1]]

        ident = const("ident")
        mask = const("mask")
        wexp = sb("wexp", [P, E * C])[:, :]
        levels = sb("levels", [MID, 2 * P])
        second = sb("second", [MID, GRP, 2])
        filt = sb("filt", [P, 3, GRP])
        eps_t = sb("eps_t", [P, 1])
        root = sb("root", [P, 1])
        zero_row = sb("zero_row", [P, ROW])
        before = sb("before", [P, P], BF16)
        ones = sb("ones", [P, P], BF16)
        warm_rows = sb("warm_rows", [P, 512], BF16)
        xb = two("xb", [P, Q, C])
        h = two("h", [P, TT * C])
        hb = two("hb", [P, TT * C])
        stats1, stats2 = two("stats1_", [P, TT, 6]), two("stats2_", [P, TT, 6])
        mv1, mv2 = two("mv1_", [P, TT, 2]), two("mv2_", [P, TT, 2])
        std1, std2 = two("std1_", [P, TT]), two("std2_", [P, TT])
        rstd1, shift1 = two("rstd1_", [P, TT]), two("shift1_", [P, TT])
        xn1 = two("xn1_", [P, TT, C])
        xT_hi, xT_lo = two("xT_hi", [P, KC, TT * P], F32R), two("xT_lo", [P, KC, TT * P], F32R)
        kv = two("kv", [P, 4, 2 * NG, GRP + 1])
        qT = two("qT", [P, KC, TT * P])
        bd = two("bd", [P, KC, 2, P + HPG])
        rden = two("rden", [P, TT, 2 * HPG])
        den = two("den", [P, TT, 2 * HPG])
        att = two("att", [P, TT, C])
        attT_hi, attT_lo = two("attT_hi", [P, KC, TT * P], F32R), two("attT_lo", [P, KC, TT * P], F32R)
        row = two("row", [P, TT, ROW])
        xn2 = two("xn2_", [P, TT, C])
        x2T = two("x2T", [P, KC, TT * P])
        wqkv = [xn2[k][:, :, :].rearrange("p t c -> p (t c)") for k in range(KC)]
        wproj = att[1][:, 0:KC, :]
        smax = two("smax", [P, TT])
        key = two("key", [P, TT * E])
        kmax = two("kmax", [P, TT])
        onehot = two("onehot", [P, TT * E], BF16)
        seen = two("seen", [P, E], BF16)
        seen_part = two("seen_part", [P, E], BF16)
        place = two("place", [P, TT * E])
        pos_sum = two("pos_sum", [P, TT])
        pos = two("pos", [P, TT], U32)
        count, part, tiles, ends, starts = (sb(n, [P, E]) for n in ("count", "part", "tiles", "ends", "starts"))
        first_row, last_row, begin = (sb(n, [P, E]) for n in ("first_row", "last_row", "begin"))
        first_jump, last_jump = sb("first_jump", [P, E]), sb("last_jump", [P, E])
        upto = sb("upto", [P, E, E])
        past, jumped, last_jumped = (sb(n, [P, TILES - EARLY, E]) for n in ("past", "jumped", "last_jumped"))
        expert, row_at, row_end, row_from, twice = (sb(n, [P, TILES - EARLY]) for n in ("expert", "row_at", "row_end", "row_from", "twice"))
        w_off, r_off = sb("w_off", [P, WLEAD + TILES + 2], I32), sb("r_off", [P, TILES + 1], I32)
        skip = sb("skip", [P, TILES])
        srow = [xb[0][:, :, :].rearrange("p q c -> p (q c)")[:, ROW * i:ROW * (i + 1)] for i in range(RING)]
        y = [xb[1][:, i, :] for i in range(RING)]
        token = [sb(f"token{i}", [P, 1], U32) for i in range(RING)]
        sxn = [xn1[i % 2][:, i // 2, :] for i in range(4)]
        sT_hi = [xT_hi[i % 2][:, :, P * (i // 2):P * (i // 2 + 1)] for i in range(4)]
        sT_lo = [xT_lo[i % 2][:, :, P * (i // 2):P * (i // 2 + 1)] for i in range(4)]

        banks = [ctx.enter_context(nc.psum_tensor(f"bank{i}", [P, 2, 512], F32)) for i in range(2)]
        conv_ps, tr_ps = banks
        conv_flat = conv_ps[:, :, :].rearrange("p a b -> p (a b)")
        total = conv_ps[:, 0, 0:E]
        conv_tiles = [conv_flat[:, t * C:(t + 1) * C] for t in range(TT)]
        b4, b5, b6, b7 = [ctx.enter_context(nc.psum_tensor(f"ps{i}", [P, 512], F32)) for i in range(4, 8)]
        first_tiles = [b6[:, 0:C], b6[:, C:2 * C], b5[:, 0:C]]

        x_loaded = [sem("x_loaded0"), sem("x_loaded1")]
        x_rest_loaded = [sem("x_rest_loaded0"), sem("x_rest_loaded1")]
        scattered = [sem("scattered0"), sem("scattered1")]
        srow_loaded = [sem(f"srow_loaded{i}") for i in range(RING)]
        y_stored = [sem(f"y_stored{i}") for i in range(RING)]
        names = """taps_loaded const_loaded bias_loaded wqkv_loaded wproj_loaded wexp_loaded margin_stored zero_ready id_start
            eps_ready kv_ones warm_rows_zero filt_ps filt_ready wqkv_hi_ready wqkv_split
            wproj_hi_ready wproj_split wexp_plus wexp_hi_ready wexp_split rank_consts
            conv_done h_ready hb_ready stats1_done var1_ready std1_ready rstd1_ready shift1_ready xn1_ready
            t1_done xT_hi_ready xT_lo_ready kv_done kv_ready q_done q0_ready q1_ready vk_done bd_ready
            vkq_done den_copied rden_ready att_ready at_done attT_hi_ready attT_lo_ready proj_done h2_ready
            stats2_done var2_ready std2_ready rstd2_ready shift2_ready xn2_ready t2_done x2T_ready
            score_done smax_ready eq_ready key_ready kmax_ready onehot_ready
            seen_parts seen_ready rank_done place_ready pos_summed pos_ready id_ready total_done plan_step rows_planned plan_ready
            sxn_ready st_done sT_hi_ready sT_lo_ready expert_done y_ready""".split()
        S = {n: sem(n) for n in names}

        block = ctx.enter_context(nc.Block())

        def run_steps(eng, step):
            step(-1, 1, 1, now=False, prev=False, old=False)
            step(0, 0, 1, prev=False, old=False)
            step(1, 1, 2, old=False)
            step(2, 0, 2)
            with eng.Fori(1, NP // 2 - 1) as i:
                step(i * 2 + 1, 1, i + 2)
                step(i * 2 + 2, 0, i + 2)
            step(NP - 1, 1, NP // 2 + 1, nxt=False)
            step(NP, 0, NP // 2 + 1, nxt=False, now=False)
            step(NP + 1, 1, NP // 2 + 2, nxt=False, now=False, prev=False)

        def run_tiles(eng, tile):
            for j in range(1, RING):
                tile(j, j % RING, j // RING)
            with eng.Fori(1, (TILES - 4) // RING) as i:
                for u in range(RING):
                    tile(i * RING + u, u, i)
            for j in range((TILES - 4) // RING * RING, TILES):
                tile(j, j % RING, j // RING)

        fetched = [0]

        def fetch(eng, n, offsets, max_val):
            fetched[0] += 1
            regs = [eng.alloc_register(f"offset{fetched[0]}_{i}") for i in range(n)]
            eng.load(regs, offsets)
            return [eng.snap(r, donate=True, min_val=0, max_val=max_val) for r in regs]

        def there(k):
            return not isinstance(k, int) or 0 <= k < TILES


        assert RING <= EARLY <= 2 * RING and 3 * RING <= TILES <= 4 * RING

        def windows(row, width, by=2):
            return bass.AP(tensor=row.tensor, offset=row.offset, ap=[[by, MID], [1, width]])

        @block.sync
        def _(sp):
            sp.dma_start(levels[:, :], windows(taps[0, :], 2 * P)).then_inc(S["taps_loaded"], 16)
            sp.dma_start(second[:, :, :], windows(taps[1, :], 2 * GRP, 1).rearrange("m (o k) -> m o k", k=2)).then_inc(S["taps_loaded"], 16)

            def load(s, a):
                xs = xp[s]
                sp.dma_start(xb[a][:, 0:Q:NJ, :], xs[0:P, :, :]).then_inc(x_loaded[a], 16)
                for b in range(2):
                    sp.dma_start(xb[a][:, NJ * b + 1:NJ * (b + 1), :],
                                 xs[FIRST:N, b, :].rearrange("(j p) c -> p j c", p=P)).then_inc((x_loaded, x_rest_loaded)[b][a], 16)

            load(0, 0)
            for k in range(KC):
                sp.dma_start(wqkv[k], wqkvT[k * P:(k + 1) * P, :]).then_inc(S["wqkv_loaded"], 16)
            sp.dma_start(consts[:, :], const_c).then_inc(S["const_loaded"], 16)
            load(1, 1)
            sp.dma_start(bias_bc[:, :], bias.rearrange("(a k) -> a k", a=1).to_broadcast([P, C])).then_inc(S["bias_loaded"], 16)
            sp.dma_start(wproj, wprojT.rearrange("(k p) o -> p k o", p=P)).then_inc(S["wproj_loaded"], 16)
            sp.dma_start(gate[:, :, :], gateT.rearrange("(k p) o -> p k o", p=P)).then_inc(S["wproj_loaded"], 16)
            sp.dma_start(wexp, wexpT[0:P, :]).then_inc(S["wexp_loaded"], 16)
            sp.wait_ge(S["zero_ready"], 1)
            margins = sorted_rows.rearrange("(e r) c -> r e c", r=REGION)[0:P, :, :]
            sp.dma_start(margins, zero_row[:, :].rearrange("p (a c) -> p a c", a=1).to_broadcast([P, E, ROW])).then_inc(S["margin_stored"], 16)

            def step(s, a):
                sp.wait_ge(S["conv_done"], s + 2)
                load(s + 3, 1 - a)

            step(-1, 1)
            step(0, 0)
            sp.wait_ge(S["wexp_split"], 1)
            sp.dma_start(wexp, wexpT[P:, :]).then_inc(S["wexp_loaded"], 16)
            with sp.Fori(0, NP // 2 - 2) as i:
                step(i * 2 + 1, 1)
                step(i * 2 + 2, 0)

            def load_rows(k0, tiles, read_before):
                starts_at = fetch(sp, tiles, r_off[0:1, bass.ds(k0, tiles)], (E - 1) * REGION + NTOK)
                for k in range(k0, k0 + tiles):
                    if read_before:
                        sp.wait_ge(S["y_ready"], k - (RING - 1))
                    sp.dma_start(srow[k % RING], sorted_rows[bass.ds(starts_at[k - k0], P), :]).then_inc(srow_loaded[k % RING], 16)

            sp.wait_ge(S["rows_planned"], 1)
            sp.wait_ge(S["margin_stored"], 16)
            for a in range(2):
                sp.wait_ge(scattered[a], 16 * TT * (NP // 2 - 1))
            load_rows(0, RING, False)
            load_rows(RING, EARLY - RING, True)
            sp.wait_ge(S["rows_planned"], 2)
            for a in range(2):
                sp.wait_ge(scattered[a], 16 * TT * NP // 2)
            load_rows(EARLY, 2 * RING - EARLY, True)
            load_rows(2 * RING, RING, True)
            load_rows(3 * RING, TILES - 3 * RING, True)

            for u in range(RING):
                sp.wait_ge(y_stored[u], 16 * ((TILES - u + RING - 1) // RING))

        @block.gpsimd
        def _(pool):
            nc.gpsimd.memset(warm_rows[:, :], 0.0).then_inc(S["warm_rows_zero"], 1)
            nc.gpsimd.memset(w_off[:, :], 0)
            nc.gpsimd.memset(r_off[:, :], 0)
            nc.gpsimd.memset(zero_row[:, :], 0.0).then_inc(S["zero_ready"], 1)
            for a in range(2):
                nc.gpsimd.memset(kv[a][:, :, :, :], 0.0).then_inc(S["kv_ones"], 1)
            pool.wait_ge(S["kv_ones"], 2)
            for a in range(2):
                nc.gpsimd.memset(kv[a][:, 0:4:3, NG:, GRP:], 1.0).then_inc(S["kv_ones"], 1)
            pool.wait_ge(S["kv_ones"], 4)
            for a in range(2):
                nc.gpsimd.memset(kv[a][0:64, 1, NG:, GRP:], 1.0).then_inc(S["kv_ones"], 1)
                nc.gpsimd.memset(kv[a][64:P, 2, NG:, GRP:], 1.0).then_inc(S["kv_ones"], 1)
            pool.wait_ge(S["kv_ones"], 8)
            nc.gpsimd.memset(ones[:, :], 1.0)
            pool.wait_ge(S["const_loaded"], 16)
            nc.gpsimd.tensor_copy(before[:, :], const("before"))
            nc.gpsimd.tensor_copy(seen[0][:, :], const("start")).then_inc(S["rank_consts"], 1)
            for a in range(2):
                nc.gpsimd.tensor_copy(row[a][:, :, TOKEN], const("ids")[:, TT * a:TT * a + TT]).then_inc(S["id_start"], 1)
            pool.wait_ge(S["id_start"], 2)
            pool.wait_ge(S["rank_consts"], 1)

            def step(s, a, turn, now=True, prev=True, nxt=True, old=True):
                n = 1 - a
                if old and not prev:
                    tile(0, 0, 0)
                if old and prev:
                    pool.wait_ge(S["onehot_ready"], s - 1)
                    if not (isinstance(s, int) and s < 3):
                        pool.wait_ge(S["rank_done"], s - 2)
                    nc.gpsimd.tensor_tensor(seen_part[0][:, :], seen[a][:, :], onehot[a][:, 0:E], ALU.add).then_inc(S["seen_parts"], 1)
                    nc.gpsimd.tensor_tensor(seen_part[1][:, :], onehot[a][:, E:2 * E], onehot[a][:, 2 * E:], ALU.add).then_inc(S["seen_parts"], 1)
                    pool.wait_ge(S["seen_parts"], 2 * (s - 1))
                    nc.gpsimd.tensor_tensor(seen[n][:, :], seen_part[0][:, :], seen_part[1][:, :], ALU.add).then_inc(S["seen_ready"], 1)
                    pool.wait_ge(S["seen_ready"], s - 1)
                if prev:
                    if not (isinstance(s, int) and s < 3):
                        pool.wait_ge(scattered[n], 16 * TT * (turn - 2))
                    pool.nop(nofuse=True)
                    nc.gpsimd.tensor_scalar_add(row[n][:, :, TOKEN], row[n][:, :, TOKEN], float(2 * TT * P)).then_inc(S["id_ready"], 1)
                if old:
                    pool.wait_ge(S["pos_ready"], s - 1)
                    pool.wait_ge(S["id_ready"], s - 1)
                    pool.nop(nofuse=True)
                    for t in range(TT):
                        pool.indirect_dma_start(sorted_rows, bass.IndirectOffsetOnAxis(ap=pos[a][:, t:t + 1], axis=0),
                                                row[a][:, t, :], None, bounds_check=E * REGION - 1, oob_is_err=False
                                                ).then_inc(scattered[a], 16)
                if isinstance(s, int) and s == -1:
                    pool.wait_ge(S["bias_loaded"], 16)
                if nxt:
                    pool.wait_ge(S["h_ready"], s + 2)
                    if prev:
                        pool.wait_ge(S["h2_ready"], 2 * s)
                    for t in range(TT):
                        ins = nc.gpsimd.tensor_tensor(hb[n][:, t * C:(t + 1) * C], h[n][:, t * C:(t + 1) * C],
                                                      bias_bc[:, :], ALU.add)
                    ins.then_inc(S["hb_ready"], 1)
                if isinstance(s, int) and s in (0, 1):
                    pool.wait_ge(S["wexp_loaded"], 16 * (s + 1))
                    own_channel = wexp.rearrange("p (e c) -> p e c", c=C)[:, :, s * P:(s + 1) * P]
                    nc.gpsimd.tensor_tensor(own_channel, own_channel, ident.rearrange("p (a c) -> p a c", a=1).to_broadcast([P, E, P]), ALU.add).then_inc(S["wexp_plus"], 1)

            def tile(j, u, turn):
                if there(j):
                    pool.wait_ge(S["y_ready"], j + 1)
                    pool.nop(nofuse=True)
                    pool.indirect_dma_start(out_rows, bass.IndirectOffsetOnAxis(ap=token[u][:, 0:1], axis=0),
                                            y[u], None, bounds_check=NTOK - 1, oob_is_err=False
                                            ).then_inc(y_stored[u], 16)

            run_steps(pool, step)

            run_tiles(pool, tile)

        @block.scalar
        def _(act):
            act.wait_ge(S["eps_ready"], 1)
            nc.scalar.activation(root[:, :], eps_t[:, :], ACT.Sqrt)
            act.wait_ge(S["filt_ps"], 1)
            nc.scalar.activation(filt[:, :, :], b4[:, 0:3 * GRP].rearrange("p (m o) -> p m o", o=GRP), ACT.Copy).then_inc(S["filt_ready"], 1)

            def norm(dst, src, rstd, shift, ready):
                for t in range(TT):
                    nc.scalar.activation(dst[:, t, :], src(t), ACT.Identity, bias=shift(t), scale=rstd(t)).then_inc(S[ready], 1)

            def second_norm(p, b):
                act.wait_ge(S["var2_ready"], p + 1)
                nc.scalar.activation(std2[b][:, :], mv2[b][:, :, 1], ACT.Sqrt, bias=eps_t[:, 0:1]).then_inc(S["std2_ready"], 1)
                act.wait_ge(S["shift2_ready"], p + 1)
                norm(xn2[b], lambda t: row[b][:, t, 0:C], lambda t: row[b][:, t, RSTD:RSTD + 1],
                     lambda t: row[b][:, t, SHIFT:SHIFT + 1], "xn2_ready")

            def x2T_out(s, a):
                act.wait_ge(S["t2_done"], s - 1)
                nc.scalar.activation(x2T[a][:, :, :], tr_ps[:, :, 0:TT * P], ACT.Copy).then_inc(S["x2T_ready"], 1)

            def experts_hi(k, part):
                cols = slice(part * E * C // 2, (part + 1) * E * C // 2)
                act.wait_ge(S["wexp_plus"], k + 1)
                nc.scalar.activation(wexp_hi[:, k, cols], wexp[:, cols], ACT.Copy).then_inc(S["wexp_hi_ready"], 1)

            def heads(ap):
                return ap.rearrange("p (g c) -> p g c", c=GRP)

            def keys_values_out(s, a, t):
                act.wait_ge(S["kv_done"], TT * s + t + 1)
                if t == 1:
                    nc.scalar.activation(kv[a][:, 1, 0:NG, 0:GRP], heads(b4[:, 0:C]), ACT.Relu)
                    nc.scalar.activation(kv[a][0:64, 1, NG:, 0:GRP], heads(b4[0:64, C:]), ACT.Relu)
                    nc.scalar.activation(kv[a][64:P, 2, NG:, 0:GRP], heads(b4[64:P, C:]), ACT.Relu).then_inc(S["kv_ready"], 1)
                else:
                    nc.scalar.activation(kv[a][:, (0, None, 3)[t], :, 0:GRP], heads((b7, None, b5)[t][:, :]), ACT.Relu).then_inc(S["kv_ready"], 1)

            def step(s, a, turn, now=True, prev=True, nxt=True, old=True):
                n = 1 - a
                if isinstance(s, int) and s == 0:
                    act.wait_ge(S["kv_ones"], 8)
                if isinstance(s, int) and s == 2:
                    experts_hi(1, 0)
                if nxt:
                    act.wait_ge(S["conv_done"], s + 2)
                    if prev:
                        act.wait_ge(S["hb_ready"], s)
                    if isinstance(s, int) and s == 0:
                        nc.scalar.activation(h[n][:, 0:2 * C], b6[:, :], ACT.Copy)
                        nc.scalar.activation(h[n][:, 2 * C:], first_tiles[2], ACT.Copy).then_inc(S["h_ready"], 1)
                    else:
                        nc.scalar.activation(h[n][:, :], conv_flat[:, 0:TT * C], ACT.Copy).then_inc(S["h_ready"], 1)
                if isinstance(s, int) and s == -1:
                    act.wait_ge(S["wqkv_loaded"], 16 * KC)
                    for k in range(KC):
                        nc.scalar.activation(wqkv_hi[:, k, :], wqkv[k], ACT.Copy).then_inc(S["wqkv_hi_ready"], 1)
                if old and now:
                    x2T_out(s, a)
                if prev:
                    for m, bank in enumerate((b4, b5)):
                        act.wait_ge(S["at_done"], KC * (s - 1) + m + 1)
                        nc.scalar.activation(attT_hi[n][:, m, :], bank[:, 0:TT * P], ACT.Copy).then_inc(S["attT_hi_ready"], 1)
                if isinstance(s, int) and s == 2:
                    experts_hi(1, 1)
                if old and not now:
                    if prev:
                        second_norm(s - 2, a)
                        tile(-4, 4, -1)
                    else:
                        tile(-2, 6, -1)
                    x2T_out(s, a)
                    if prev:
                        tile(-3, 5, -1)
                    else:
                        tile(-1, 7, -1)
                        tile(0, 0, 0)
                if isinstance(s, int) and s in (0, 1):
                    keys_values_out(s, a, 0)
                if nxt:
                    act.wait_ge(S["var1_ready"], s + 2)
                    nc.scalar.activation(std1[n][:, :], mv1[n][:, :, 1], ACT.Sqrt, bias=eps_t[:, 0:1]).then_inc(S["std1_ready"], 1)
                if isinstance(s, int) and s in (0, 1):
                    keys_values_out(s, a, 1)
                if nxt:
                    act.wait_ge(S["shift1_ready"], s + 2)
                    norm(xn1[n], lambda t: h[n][:, t * C:(t + 1) * C], lambda t: rstd1[n][:, t:t + 1],
                         lambda t: shift1[n][:, t:t + 1], "xn1_ready")
                if now:
                    for t in range(TT):
                        if t == 2 or not (isinstance(s, int) and s in (0, 1)):
                            keys_values_out(s, a, t)
                    act.wait_ge(S["q_done"], KC * s + 1)
                    nc.scalar.activation(qT[a][:, 0, :], b6[:, 0:TT * P], ACT.Relu).then_inc(S["q0_ready"], 1)
                    act.wait_ge(S["q_done"], KC * s + 2)
                    nc.scalar.activation(qT[a][:, 1, :], b7[:, 0:TT * P], ACT.Relu).then_inc(S["q1_ready"], 1)
                if nxt:
                    act.wait_ge(S["t1_done"], s + 2)
                    nc.scalar.activation(xT_hi[n][:, :, :], tr_ps[:, :, 0:TT * P], ACT.Copy).then_inc(S["xT_hi_ready"], 1)
                if isinstance(s, int) and s == 0:
                    act.wait_ge(S["wproj_loaded"], 32)
                    nc.scalar.activation(wproj_hi[:, :, :], wproj, ACT.Copy).then_inc(S["wproj_hi_ready"], 1)
                    experts_hi(0, 0)
                    experts_hi(0, 1)
                if prev and (nxt or not now):
                    second_norm(s - 1, n)

            def tile(j, u, turn):
                if there(j + 2):
                    v = (u + 2) % 4
                    act.wait_ge(S["st_done"], j + 3)
                    nc.scalar.activation(sT_hi[v], (b4, b5)[v % 2][:, 0:C].rearrange("p (k t) -> p k t", k=KC), ACT.Copy).then_inc(S["sT_hi_ready"], 1)
                if there(j + 4):
                    r, v = (u + 4) % RING, u % 4
                    act.wait_ge(srow_loaded[r], 16 * (turn + 1 + (u + 4) // RING))
                    nc.scalar.activation(sxn[v], srow[r][:, 0:C], ACT.Identity, bias=srow[r][:, SHIFT:SHIFT + 1],
                                         scale=srow[r][:, RSTD:RSTD + 1]).then_inc(S["sxn_ready"], 1)

            run_steps(act, step)

            run_tiles(act, tile)

        @block.vector
        def _(dve):
            nc.vector.memset(eps_t[:, :], EPS).then_inc(S["eps_ready"], 1)
            for jump in (first_jump, last_jump):
                nc.vector.memset(jump[:, E - 1:], 0.0)
            nc.vector.memset(skip[:, 0:EARLY], 0.0)

            def stats(src, st, done):
                for t in range(TT):
                    nc.vector.bn_stats(st[:, t, :], src(t)).then_inc(S[done], 1)

            def mean_var(st, mv, cnt, done, ready):
                dve.wait_ge(S[done], TT * cnt)
                dve.nop(nofuse=True)
                for t in range(TT):
                    ins = nc.vector.bn_aggr(mv[:, t, :], st[:, t, :])
                ins.then_inc(S[ready], 1)

            def rstd_shift(mv, std, rstd, shift, cnt, std_ready, rstd_ready, shift_ready):
                dve.wait_ge(S[std_ready], cnt)
                nc.vector.reciprocal(rstd, std[:, :]).then_inc(S[rstd_ready], 1)
                dve.wait_ge(S[rstd_ready], cnt)
                nc.vector.scalar_tensor_tensor(shift, mv[:, :, 0], -1.0, rstd, ALU.mult, ALU.mult).then_inc(S[shift_ready], 1)

            def second_rstd_shift(p, b):
                rstd_shift(mv2[b], std2[b], row[b][:, :, RSTD], row[b][:, :, SHIFT], p + 1, "std2_ready", "rstd2_ready", "shift2_ready")

            def divide(s, a):
                nds = [bank[:, 0:KC * (P + HPG)].rearrange("p (m e) -> p m e", e=P + HPG) for bank in (b7, b4, b5)]
                for t, nd in enumerate(nds):
                    dve.wait_ge(S["vkq_done"], TT * s + t + 1)
                    nc.vector.tensor_scalar_add(den[a][:, t, :].rearrange("p (m e) -> p m e", e=HPG), nd[:, :, P:], DEN_EPS).then_inc(S["den_copied"], 1)
                for t in range(TT):
                    dve.wait_ge(S["den_copied"], TT * s + t + 1)
                    nc.vector.reciprocal(rden[a][:, t, :], den[a][:, t, :]).then_inc(S["rden_ready"], 1)
                for t, nd in enumerate(nds):
                    dve.wait_ge(S["rden_ready"], TT * s + t + 1)
                    ins = nc.vector.tensor_tensor(
                        att[a][:, t, :].rearrange("p (m g e) -> p m g e", m=KC, e=HD),
                        nd[:, :, 0:P].rearrange("p m (g e) -> p m g e", e=HD),
                        rden[a][:, t, :].rearrange("p (m g o) -> p m g o", m=KC, o=1).to_broadcast([P, KC, HPG, HD]),
                        ALU.mult)
                    ins.then_inc(S["att_ready"], 1)

            def choose(s, a):
                sc3 = b6[:, 0:TT * E].rearrange("p (t e) -> p t e", e=E)
                k3 = key[a][:, :].rearrange("p (t e) -> p t e", e=E)
                o3 = onehot[a][:, :].rearrange("p (t e) -> p t e", e=E)

                def spread(v):
                    return v[:, :].rearrange("p (t o) -> p t o", o=1).to_broadcast([P, TT, E])
                dve.wait_ge(S["score_done"], s - 1)
                nc.vector.tensor_reduce(smax[a][:, :], sc3, AX_X, ALU.max).then_inc(S["smax_ready"], 1)
                dve.wait_ge(S["smax_ready"], s - 1)
                nc.vector.tensor_tensor(k3, sc3, spread(smax[a]), ALU.is_equal).then_inc(S["eq_ready"], 1)
                dve.wait_ge(S["eq_ready"], s - 1)
                nc.vector.tensor_tensor(key[a][:, :], key[a][:, :], const("tie"), ALU.mult).then_inc(S["key_ready"], 1)
                dve.wait_ge(S["key_ready"], s - 1)
                nc.vector.tensor_reduce(kmax[a][:, :], k3, AX_X, ALU.max).then_inc(S["kmax_ready"], 1)
                dve.wait_ge(S["kmax_ready"], s - 1)
                nc.vector.tensor_tensor(o3, k3, spread(kmax[a]), ALU.is_equal).then_inc(S["onehot_ready"], 1)

            def places(s, a):
                dve.wait_ge(S["rank_done"], s - 1)
                nc.vector.tensor_tensor(place[a][:, :], conv_ps[:, 1, RANK:RANK + TT * E], onehot[a][:, :], ALU.mult).then_inc(S["place_ready"], 1)
                dve.wait_ge(S["place_ready"], s - 1)
                nc.vector.tensor_reduce(pos_sum[a][:, :], place[a][:, :].rearrange("p (t e) -> p t e", e=E), AX_X, ALU.add).then_inc(S["pos_summed"], 1)
                dve.wait_ge(S["pos_summed"], s - 1)
                nc.vector.tensor_copy(pos[a][:, :], pos_sum[a][:, :]).then_inc(S["pos_ready"], 1)

            links = [0]

            def link(ins):
                links[0] += 1
                ins.then_inc(S["plan_step"], 1)
                dve.wait_ge(S["plan_step"], links[0])

            def over(v, n, m):
                return v.rearrange("p (a m) -> p a m", a=1).to_broadcast([P, n, m])

            def each(v, n, m):
                return v.rearrange("p (n a) -> p n a", a=1).to_broadcast([P, n, m])

            def plan_ends(n, begins, half, turn):
                dve.wait_ge(S["total_done"], turn)
                nc.vector.tensor_scalar_add(last_row[:, :], total, -float(P))
                link(nc.vector.tensor_tensor(count[:, :], total, begins, ALU.subtract))
                link(nc.vector.tensor_scalar(part[:, :], count[:, :], 1.0 / P, half, ALU.mult, ALU.add))
                link(nc.vector.tensor_scalar(tiles[:, :], part[:, :], ROUND, ROUND, ALU.add, ALU.subtract))
                link(nc.vector.tensor_tensor(upto[:, :, :], over(tiles[:, :], E, E), const("upto").rearrange("p (e f) -> p e f", f=E), ALU.mult))
                link(nc.vector.tensor_reduce(ends[:, :], upto[:, :, :], AX_X, ALU.add))
                nc.vector.tensor_tensor(past[:, 0:n, :], over(ends[:, :], n, E), each(const("tile")[:, 0:n], n, E), ALU.is_le)
                link(nc.vector.tensor_tensor(starts[:, :], ends[:, :], tiles[:, :], ALU.subtract))

            def plan_jumps(begins):
                link(nc.vector.scalar_tensor_tensor(first_row[:, :], starts[:, :], -float(P), begins, ALU.mult, ALU.add))
                link(nc.vector.tensor_tensor(first_jump[:, 0:E - 1], first_row[:, 1:], first_row[:, 0:E - 1], ALU.subtract))

            def plan_rows(n):
                link(nc.vector.tensor_tensor(jumped[:, 0:n, :], past[:, 0:n, :], over(first_jump[:, :], n, E), ALU.mult))
                link(nc.vector.tensor_reduce(row_at[:, 0:n], jumped[:, 0:n, :], AX_X, ALU.add))
                link(nc.vector.scalar_tensor_tensor(row_at[:, 0:n], row_at[:, 0:n], first_row[:, 0:1], const("rows")[:, 0:n], ALU.add, ALU.add))

            def plan_weights(n, first, turn):
                link(nc.vector.tensor_reduce(expert[:, 0:n], past[:, 0:n, :], AX_X, ALU.add))
                nc.vector.tensor_scalar(w_off[:, WLEAD + first:WLEAD + first + n], expert[:, 0:n], float(E - 1), float(C), ALU.min, ALU.mult).then_inc(S["plan_ready"], 1)

            def plan_early_offsets():
                nc.vector.tensor_copy(r_off[:, 0:EARLY], row_at[:, 0:EARLY]).then_inc(S["rows_planned"], 1)

            def plan_early_weights():
                plan_weights(EARLY, 0, 1)
                link(nc.vector.tensor_scalar_min(starts[:, :], starts[:, :], float(EARLY)))
                link(nc.vector.scalar_tensor_tensor(tiles[:, :], ends[:, :], float(EARLY), starts[:, :], ALU.min, ALU.subtract))
                link(nc.vector.scalar_tensor_tensor(begin[:, :], tiles[:, :], float(P), const("base"), ALU.mult, ALU.add))

            def plan_late_ends():
                link(nc.vector.tensor_tensor(last_jump[:, 0:E - 1], last_row[:, 1:], last_row[:, 0:E - 1], ALU.subtract))
                link(nc.vector.tensor_tensor(last_jumped[:, :, :], past[:, :, :], over(last_jump[:, :], TILES - EARLY, E), ALU.mult))
                link(nc.vector.tensor_reduce(row_end[:, :], last_jumped[:, :, :], AX_X, ALU.add))

            def plan_late_offsets():
                link(nc.vector.scalar_tensor_tensor(row_from[:, :], row_end[:, :], last_row[:, 0:1], row_at[:, :], ALU.add, ALU.min))
                nc.vector.tensor_copy(r_off[:, EARLY:TILES], row_from[:, :]).then_inc(S["rows_planned"], 1)

            def plan_late_skips():
                link(nc.vector.tensor_tensor(twice[:, :], row_at[:, :], row_from[:, :], ALU.subtract))
                link(nc.vector.tensor_scalar(skip[:, EARLY:TILES], twice[:, :], const("lane"), float(BIG), ALU.is_gt, ALU.mult))

            def attention_lo(s, a):
                for m, bank in enumerate((b4, b5)):
                    dve.wait_ge(S["attT_hi_ready"], KC * s + m + 1)
                    nc.vector.tensor_tensor(attT_lo[a][:, m, :], bank[:, 0:TT * P], attT_hi[a][:, m, :].bitcast(F32), ALU.subtract).then_inc(S["attT_lo_ready"], 1)

            def step(s, a, turn, now=True, prev=True, nxt=True, old=True):
                n = 1 - a
                if isinstance(s, int) and s == 1:
                    attention_lo(s - 1, n)
                if nxt:
                    dve.wait_ge(S["h_ready"], s + 2)
                    stats(lambda t: h[n][:, t * C:(t + 1) * C], stats1[n], "stats1_done")
                    mean_var(stats1[n], mv1[n], s + 2, "stats1_done", "var1_ready")
                if prev and not (isinstance(s, int) and s == 1):
                    attention_lo(s - 1, n)
                if prev and old and not now:
                    second_rstd_shift(s - 2, a)
                if nxt:
                    rstd_shift(mv1[n], std1[n], rstd1[n][:, :], shift1[n][:, :], s + 2, "std1_ready", "rstd1_ready", "shift1_ready")
                if old and now:
                    choose(s, a)
                    places(s, a)
                    if not nxt:
                        plan_ends(EARLY, const("base"), -HALF, 1)
                        plan_jumps(const("base"))
                        plan_rows(EARLY)
                        plan_early_offsets()
                if isinstance(s, int) and s in (1, 2):
                    k = s - 1
                    dve.wait_ge(S["wexp_hi_ready"], 2 * (k + 1))
                    nc.vector.tensor_tensor(wexp_lo[:, k, :], wexp, wexp_hi[:, k, :].bitcast(F32), ALU.subtract).then_inc(S["wexp_split"], 1)
                if now:
                    dve.wait_ge(S["vk_done"], s + 1)
                    vk = b6[:, 0:4 * (GRP + 1)].rearrange("p (i e) -> p i e", e=GRP + 1)
                    bd_all = bd[a][:, :, :, :].rearrange("p m b e -> p (m b) e")
                    nc.vector.tensor_tensor(bd_all[:, :, 0:P].rearrange("p i (g e) -> p i g e", e=GRP),
                                            vk[:, :, 0:GRP].rearrange("p i (a e) -> p i a e", a=1).to_broadcast([P, 4, P // GRP, GRP]),
                                            mask[:, 0:P].rearrange("p (a g e) -> p a g e", a=1, e=GRP).to_broadcast([P, 4, P // GRP, GRP]), ALU.mult)
                    nc.vector.tensor_tensor(bd_all[:, :, P:], mask[:, P:].rearrange("p (a e) -> p a e", a=1).to_broadcast([P, 4, HPG]),
                                            vk[:, :, GRP:].to_broadcast([P, 4, HPG]), ALU.mult).then_inc(S["bd_ready"], 1)
                if prev:
                    dve.wait_ge(S["hb_ready"], s)
                    if not (isinstance(s, int) and s < 3):
                        dve.wait_ge(scattered[n], 16 * TT * (turn - 2))
                    dve.wait_ge(S["proj_done"], 2 * s - 1)
                    nc.vector.tensor_tensor(row[n][:, 0:2, 0:C], b4[:, :].rearrange("p (t c) -> p t c", c=C),
                                            hb[n][:, 0:2 * C].rearrange("p (t c) -> p t c", c=C), ALU.add).then_inc(S["h2_ready"], 1)
                    dve.wait_ge(S["proj_done"], 2 * s)
                    nc.vector.tensor_tensor(row[n][:, 2, 0:C], b5[:, 0:C], hb[n][:, 2 * C:3 * C], ALU.add).then_inc(S["h2_ready"], 1)
                    dve.wait_ge(S["h2_ready"], 2 * s)
                    stats(lambda t: row[n][:, t, 0:C], stats2[n], "stats2_done")
                if now and not nxt:
                    divide(s, a)
                    plan_early_weights()
                if prev:
                    mean_var(stats2[n], mv2[n], s, "stats2_done", "var2_ready")
                if isinstance(s, int) and s == -1:
                    for k in range(KC):
                        dve.wait_ge(S["wqkv_hi_ready"], k + 1)
                        nc.vector.tensor_tensor(wqkv_lo[:, k, :], wqkv[k], wqkv_hi[:, k, :].bitcast(F32), ALU.subtract).then_inc(S["wqkv_split"], 1)
                    dve.wait_ge(S["const_loaded"], 16)
                if nxt:
                    dve.wait_ge(S["xT_hi_ready"], s + 2)
                    nc.vector.tensor_tensor(xT_lo[n][:, :, :], tr_ps[:, :, 0:TT * P], xT_hi[n][:, :, :].bitcast(F32), ALU.subtract).then_inc(S["xT_lo_ready"], 1)
                if isinstance(s, int) and s == 0:
                    dve.wait_ge(S["wproj_hi_ready"], 1)
                    nc.vector.tensor_tensor(wproj_lo[:, :, :], wproj, wproj_hi[:, :, :].bitcast(F32), ALU.subtract).then_inc(S["wproj_split"], 1)
                if prev and (nxt or not now):
                    second_rstd_shift(s - 1, n)
                if old and not now:
                    if not prev:
                        tile(-1, 7, -1)
                        tile(0, 0, 0)
                    choose(s, a)
                    places(s, a)
                    if prev:
                        tile(-2, 6, -1)
                if now and nxt:
                    divide(s, a)

            def tile(j, u, turn):
                if isinstance(j, int) and j == 1:
                    plan_ends(TILES - EARLY, begin[:, :], HALF, 2)
                if isinstance(j, int) and j == 2:
                    plan_jumps(begin[:, :])
                if isinstance(j, int) and j == 3:
                    plan_rows(TILES - EARLY)
                if isinstance(j, int) and j == 4:
                    plan_late_ends()
                if isinstance(j, int) and j == 5:
                    plan_late_offsets()
                if isinstance(j, int) and j == 6:
                    plan_late_skips()
                if isinstance(j, int) and j == 7:
                    plan_weights(TILES - EARLY, EARLY, 2)
                if there(j + 2):
                    v = (u + 2) % 4
                    dve.wait_ge(S["sT_hi_ready"], j + 3)
                    nc.vector.tensor_tensor(sT_lo[v], (b4, b5)[v % 2][:, 0:C].rearrange("p (k t) -> p k t", k=KC),
                                            sT_hi[v].bitcast(F32), ALU.subtract).then_inc(S["sT_lo_ready"], 1)
                if there(j):
                    if not (isinstance(j, int) and j < RING):
                        dve.wait_ge(y_stored[u], 16 * turn)
                    nc.vector.tensor_tensor(token[u][:, :], srow[u][:, TOKEN:TOKEN + 1], skip[:, bass.ds(j, 1)], ALU.add)
                    dve.wait_ge(S["expert_done"], j + 1)
                    nc.vector.tensor_tensor(y[u], (b7, b6)[u % 2][:, 0:C], srow[u][:, 0:C], ALU.add).then_inc(S["y_ready"], 1)

            run_steps(dve, step)

            run_tiles(dve, tile)

        @block.tensor
        def _(pe):
            def warm_up(n, bank=b7):
                for _ in range(n):
                    nc.tensor.matmul(bank[:, :], warm_rows[:, 0:P], warm_rows[:, :], start=True, stop=True)

            pe.wait_ge(S["warm_rows_zero"], 1)
            warm_up(5)
            pe.wait_ge(S["taps_loaded"], 32)
            nc.tensor.matmul(b4[:, 0:GRP], levels[:, LEAD:LEAD + P], second[:, :, 0], start=True, stop=True)
            warm_up(1)
            nc.tensor.matmul(b4[:, GRP:2 * GRP], levels[:, 0:P], second[:, :, 0], start=True, stop=True)
            warm_up(1)
            nc.tensor.matmul(b4[:, 2 * GRP:3 * GRP], levels[:, P:2 * P], second[:, :, 0], start=True, stop=True).then_inc(S["filt_ps"], 1)
            warm_up(3)
            pe.wait_ge(S["filt_ready"], 1)

            def conv(a, load, tiles):
                pe.wait_ge(x_loaded[a], 32 * load)

                def rows(q, further):
                    t, g = divmod(q, 4)
                    inner = 0 < q % NJ < NJ - 1
                    return nc.tensor.matmul(tiles[t][GRP * g:GRP * (g + 1), :],
                                            filt[:, 2 if further else 0 if q % NJ == 0 else 1, :],
                                            xb[a][:, q + 1 if further else q, :], start=not further,
                                            stop=further or not inner, tile_position=(0, GRP * g))

                for q, further in [(0, 0), (1, 0), (2, 0), (3, 0), (4, 0), (1, 1), (2, 1), (3, 1), (4, 1), (5, 0),
                                   (6, 0), (7, 0), (8, 0), (9, 0), (10, 0), (11, 0), (8, 1), (9, 1), (10, 1), (7, 1)]:
                    if (q, further) == (NJ, 0):
                        pe.wait_ge(x_rest_loaded[a], 16 * load)
                    ins = rows(q, bool(further))
                ins.then_inc(S["conv_done"], 1)

            def flip(dst, src, s_ready, base):
                for t in range(TT):
                    pe.wait_ge(S[s_ready], base + t + 1)
                    for m in range(KC):
                        ins = nc.tensor.transpose(dst(m)[:, t * P:(t + 1) * P], src[:, t, m * P:(m + 1) * P], ident)
                return ins

            def split_product(o, lhsT, rhs):
                terms = [(l, r, k) for k in range(KC) for l, r in ((0, 0), (0, 1), (1, 0))]
                for i, (l, r, k) in enumerate(terms):
                    ins = nc.tensor.matmul(o, lhsT[l](k), rhs[r](k), start=i == 0, stop=i == len(terms) - 1)
                return ins

            def second_norm_flip(s, a):
                flip(lambda m: tr_ps[:, m, :], xn2[a], "xn2_ready", TT * (s - 2)).then_inc(S["t2_done"], 1)

            def scores(s, a):
                pe.wait_ge(S["x2T_ready"], s - 1)
                for t in range(TT):
                    for k in range(KC):
                        ins = nc.tensor.matmul(b6[:, t * E:(t + 1) * E], x2T[a][:, k, t * P:(t + 1) * P], gate[:, k, :],
                                               start=k == 0, stop=k == KC - 1)
                ins.then_inc(S["score_done"], 1)

            def keys_values(s, a, t, bank):
                split_product(bank[:, :], [lambda k, x=x: x[:, k, t * P:(t + 1) * P] for x in (xT_hi[a], xT_lo[a])],
                              [lambda k, w=w: w[:, k, C:] for w in (wqkv_hi, wqkv_lo)]).then_inc(S["kv_done"], 1)

            def ranks(s, a):
                pe.wait_ge(S["onehot_ready"], s - 1)
                if not (isinstance(s, int) and s < 3):
                    pe.wait_ge(S["seen_ready"], s - 2)
                o = conv_ps[:, 1, RANK:RANK + TT * E]
                nc.tensor.matmul(o, before[:, :], onehot[a][:, :], start=True, stop=False)
                nc.tensor.matmul(o.rearrange("p (t e) -> p t e", e=E), ones[:, :],
                                 seen[a][:, :].rearrange("p (t e) -> p t e", t=1).to_broadcast([P, TT, E]), start=False, stop=False)
                nc.tensor.matmul(o[:, E:].rearrange("p (t e) -> p t e", e=E), ones[:, :],
                                 onehot[a][:, 0:E].rearrange("p (t e) -> p t e", t=1).to_broadcast([P, TT - 1, E]), start=False, stop=False)
                nc.tensor.matmul(o[:, 2 * E:], ones[:, :], onehot[a][:, E:2 * E], start=False, stop=True).then_inc(S["rank_done"], 1)

            def totals(a):
                pe.wait_ge(S["h_ready"], NP)
                nc.tensor.matmul(total, ones[:, :], seen[a][:, :], start=True, stop=False)
                for t in range(TT):
                    ins = nc.tensor.matmul(total, ones[:, :], onehot[a][:, t * E:(t + 1) * E], start=False, stop=t == TT - 1)
                ins.then_inc(S["total_done"], 1)

            def attention_flip(s, a):
                pe.wait_ge(S["att_ready"], TT * (s + 1))
                for m, bank in enumerate((b4, b5)):
                    for t in range(TT):
                        ins = nc.tensor.transpose(bank[:, t * P:(t + 1) * P], att[a][:, t, m * P:(m + 1) * P], ident)
                    ins.then_inc(S["at_done"], 1)

            def step(s, a, turn, now=True, prev=True, nxt=True, old=True):
                n = 1 - a
                if isinstance(s, int) and s == -1:
                    conv(0, 1, conv_tiles)
                    warm_up(17)
                    pe.wait_ge(S["const_loaded"], 16)
                elif nxt and not (isinstance(s, int) and s == 0):
                    pe.wait_ge(S["h_ready"], s + 1)
                    if not (isinstance(s, int) and s < 3):
                        pe.wait_ge(S["place_ready"], s - 2)
                    conv(n, turn, conv_tiles)
                if now and not nxt:
                    pe.wait_ge(S["h_ready"], s + 1)
                if old and now:
                    pe.wait_ge(S["xT_lo_ready"], s + 1)
                    if not nxt:
                        warm_up(7, conv_ps[:, 0, :])
                    second_norm_flip(s, a)
                if isinstance(s, int) and s == 1:
                    attention_flip(s - 1, n)
                if now:
                    if isinstance(s, int) and s == 0:
                        pe.wait_ge(S["wqkv_split"], KC)
                    pe.wait_ge(S["xT_lo_ready"], s + 1)
                    if prev:
                        pe.wait_ge(S["att_ready"], TT * (s - 1) + 1)
                    keys_values(s, a, 0, b7)
                if prev and not (isinstance(s, int) and s == 1):
                    if not now:
                        warm_up(9, b6)
                    attention_flip(s - 1, n)
                if old and not now and not prev:
                    second_norm_flip(s, a)
                    pe.wait_ge(S["wexp_split"], KC)
                    tile(-1, 7, -1)
                if now:
                    if old:
                        scores(s, a)
                    if isinstance(s, int) and s == 0:
                        pe.wait_ge(S["h_ready"], 2)
                    for t, bank in enumerate((b4, b5)):
                        if prev:
                            pe.wait_ge(S["attT_lo_ready"], KC * (s - 1) + t + 1)
                        keys_values(s, a, t + 1, bank)
                    if old:
                        if nxt:
                            pe.wait_ge(S["h_ready"], s + 2)
                        ranks(s, a)
                        if not nxt:
                            totals(a)
                    for m, bank in enumerate((b6, b7)):
                        if m == 0 and old:
                            pe.wait_ge(S["eq_ready"], s - 1)
                        if m == 1:
                            pe.wait_ge(S["kv_ready"], TT * s + 1)
                        split_product(bank[:, 0:TT * P], [lambda k, w=w: w[:, k, m * P:(m + 1) * P] for w in (wqkv_hi, wqkv_lo)],
                                      [lambda k, x=x: x[:, k, :] for x in (xT_hi[a], xT_lo[a])]).then_inc(S["q_done"], 1)
                    pe.wait_ge(S["kv_ready"], TT * s + TT)
                    pe.wait_ge(S["q0_ready"], s + 1)
                    for m in range(KC):
                        for k in range(3):
                            seg, vs, first, last = ((1, slice(1, 3), 0, 2), (0, 0, 0, 1), (3, 3, 1, 2))[k]
                            for g in range(4):
                                ins = nc.tensor.matmul(b6[GRP * g:GRP * (g + 1), (2 * m + first) * (GRP + 1):(2 * m + last) * (GRP + 1)],
                                                       kv[a][:, seg, 4 * m + g, 0:GRP], kv[a][:, vs, NG + 4 * m + g, :],
                                                       start=k == 0, stop=k == 2, tile_position=(0, GRP * g))
                    ins.then_inc(S["vk_done"], 1)
                elif old and not prev:
                    scores(s, a)
                    warm_up(5, tr_ps[:, 0, :])
                if prev:
                    if not now:
                        warm_up(7, b6)
                    if isinstance(s, int) and s == 1:
                        pe.wait_ge(S["wproj_split"], 1)
                    pe.wait_ge(S["attT_lo_ready"], KC * s)
                    for t in range(TT):
                        o = b4[:, t * C:(t + 1) * C] if t < 2 else b5[:, 0:C]
                        ins = split_product(o, [lambda k, x=x: x[:, k, t * P:(t + 1) * P] for x in (attT_hi[n], attT_lo[n])],
                                            [lambda k, w=w: w[:, k, :] for w in (wproj_hi, wproj_lo)])
                        if t > 0:
                            ins.then_inc(S["proj_done"], 1)
                if old and not now:
                    if prev:
                        second_norm_flip(s, a)
                        warm_up(4, b7)
                        scores(s, a)
                        pe.wait_ge(S["plan_ready"], 1)
                        offsets[RING - 1:] = fetch(pe, 1, w_off[0:1, WLEAD:WLEAD + 1], (E - 1) * C)
                        pe.wait_ge(S["h2_ready"], 2 * NP)
                        tile(-3, 5, -1)
                        tile(-2, 6, -1)
                        warm_up(3, b7)
                    ranks(s, a)
                    if not prev:
                        totals(a)
                        tile(0, 0, 0)
                if nxt:
                    flip(lambda m: tr_ps[:, m, :], xn1[n], "xn1_ready", TT * (s + 1)).then_inc(S["t1_done"], 1)
                if isinstance(s, int) and s == -1:
                    warm_up(4)
                    conv(1, 1, first_tiles)
                    pe.wait_ge(S["rank_consts"], 1)
                if now:
                    pe.wait_ge(S["bd_ready"], s + 1)
                    pe.wait_ge(S["q1_ready"], s + 1)
                    for t, bank in enumerate((b7, b4, b5)):
                        if prev and t > 0:
                            pe.wait_ge(S["h2_ready"], 2 * (s - 1) + t)
                        for m in range(KC):
                            o = bank[:, m * (P + HPG):(m + 1) * (P + HPG)]
                            if t == 1:
                                for b in range(2):
                                    ins = nc.tensor.matmul(o[64 * b:64 * b + 64, :], qT[a][:, m, P + 64 * b:P + 64 * b + 64],
                                                           bd[a][:, m, b, :], start=True, stop=True, tile_position=(0, 64 * b))
                            else:
                                ins = nc.tensor.matmul(o, qT[a][:, m, t * P:(t + 1) * P], bd[a][:, m, t // 2, :],
                                                       start=True, stop=True)
                        ins.then_inc(S["vkq_done"], 1)

            offsets = [None] * RING

            def tile(j, u, turn):
                if there(j + 3):
                    v = (u + 3) % 4
                    pe.wait_ge(S["sxn_ready"], j + 4)
                    if not (isinstance(j, int) and j < -1):
                        pe.wait_ge(S["sT_lo_ready"], j + 2)
                    for m in range(KC):
                        ins = nc.tensor.transpose((b4, b5)[v % 2][:, m * P:(m + 1) * P], sxn[v][:, m * P:(m + 1) * P], ident)
                    ins.then_inc(S["st_done"], 1)
                if there(j + 1):
                    if u == 0:
                        if not (isinstance(j, int) and j == 0):
                            pe.wait_ge(S["plan_ready"], 2)
                        offsets[:] = fetch(pe, RING, w_off[0:1, bass.ds(WLEAD + 1 + j, RING)], (E - 1) * C)
                    v = (u + 1) % 4
                    off = offsets[u]
                    if not (isinstance(j, int) and j < 1):
                        pe.wait_ge(S["y_ready"], j)
                    pe.wait_ge(S["sT_lo_ready"], j + 2)
                    split_product((b7, b6)[v % 2][:, 0:C], [lambda k, x=x: x[:, k, :] for x in (sT_hi[v], sT_lo[v])],
                                  [lambda k, x=x: x[:, k, bass.ds(off, C)] for x in (wexp_hi, wexp_lo)]).then_inc(S["expert_done"], 1)

            run_steps(pe, step)

            run_tiles(pe, tile)


_INS = ['x', 'L0_tok_h0', 'L0_attn_qkv_weight', 'L0_attn_proj_weight', 'L0_attn_proj_bias', 'L0_ffn_gate_w', 'L0_ffn_expert_w']
_OUTS = [((16, 192, 256), 'float32')]


def kernel(**inputs):
    import numpy as _np
    import concourse.bacc as _bacc
    from concourse import mybir as _mybir
    from concourse.bass_utils import run_bass_kernel_spmd as _run

    mid = 2 * (GRP - 1) + TAPS
    taps = _np.zeros((2, 2 * (mid - 1) + 2 * P), _np.float32)
    taps[0, 2 * (mid - 1):2 * (mid - 1) + TAPS] = inputs["L0_tok_h0"]
    taps[1, mid - TAPS:mid] = inputs["L0_tok_h0"][::-1]
    put = {
        "x": inputs["x"],
        "taps": taps,
        "wqkvT": _np.transpose(inputs["L0_attn_qkv_weight"]),
        "wprojT": _np.transpose(inputs["L0_attn_proj_weight"]),
        "bias": inputs["L0_attn_proj_bias"],
        "gateT": _np.transpose(inputs["L0_ffn_gate_w"]),
        "wexpT": _np.transpose(inputs["L0_ffn_expert_w"], (2, 0, 1)).reshape(C, E * C),
    }
    lane = _np.arange(P)[:, None]
    e = _np.arange(E)
    columns = {
        "ident": lane == _np.arange(P),
        "mask": _np.concatenate([lane // HD == _np.arange(P) // HD, lane // HD == _np.arange(P // HD)], axis=1),
        "tie": _np.tile(_np.arange(E, 0, -1), 3),
        "ids": lane + P * _np.arange(6) - 6 * P,
        "start": e * (REGION // P) + 1,
        "before": lane < _np.arange(P),
        "upto": (_np.arange(E)[None, :] <= e[:, None]).reshape(-1),
        "tile": _np.arange(TILES),
        "rows": P * _np.arange(TILES),
        "base": e * REGION + P,
        "lane": lane,
    }
    packed = _np.zeros((P, NCONST), _np.float32)
    for name, (lo, hi) in CONSTS.items():
        packed[:, lo:hi] = columns[name]
    put["const_c"] = packed

    nc = _bacc.Bacc("TRN2", target_bir_lowering=False, num_devices=1)
    arrays, args = {}, []
    for name, a in put.items():
        a = _np.ascontiguousarray(a)
        arrays[f"in_{name}_dram"] = a
        args.append(nc.dram_tensor(f"in_{name}_dram", a.shape, _mybir.dt.from_np(a.dtype), kind="ExternalInput").ap())
    for i, (shape, dtype) in enumerate(_OUTS):
        dt = _mybir.dt.from_np(_np.dtype(dtype))
        args.append(nc.dram_tensor(f"out_{i}_dram", shape, dt, kind="ExternalOutput").ap())
    audio_tower(nc, *args)
    r = _run(nc, [arrays], core_ids=[0])
    return r.results[0]["out_0_dram"]
```
